# Optimizing a Trainium2 kernel written in Bass

```python
import numpy as np
import jax
import jax.numpy as jnp

def _softmax(x, axis=-1):
    return jax.nn.softmax(x, axis=axis)

def _gelu(x):
    return jax.nn.gelu(x, approximate=True)

def _silu(x):
    return jax.nn.silu(x)

def _sigmoid(x):
    return jax.nn.sigmoid(x)

def _layernorm(x, axis=-1, eps=1e-05):
    m = jnp.mean(x, axis=axis, keepdims=True)
    v = jnp.var(x, axis=axis, keepdims=True)
    return (x - m) / jnp.sqrt(v + eps)

def _scatter_add(tgt, idx, src, axis=0):
    return tgt.at[idx].add(src)

def _segment_sum(src, seg, n):
    return jax.ops.segment_sum(src, seg, n)
kernel_name = 'mk_prb_d2_jaxref_r8_03e24e'

def setup_inputs(seed: int=0):
    np.random.seed(seed)
    _w = jnp.asarray

    def _L0_attn_setup():
        import jax, jax.numpy as jnp
        import numpy as np
        EMBED = 128
        HEADS = 16
        HEAD_DIM = EMBED // HEADS
        key = jax.random.key(seed)
        ks = jax.random.split(key, 9)
        s = 1.0 / np.sqrt(EMBED)
        x = jax.random.normal(ks[0], (2, 256, EMBED), dtype=jnp.float32)
        Wq = jax.random.uniform(ks[1], (EMBED, EMBED), jnp.float32, -s, s)
        bq = jax.random.uniform(ks[2], (EMBED,), jnp.float32, -s, s)
        Wk = jax.random.uniform(ks[3], (EMBED, EMBED), jnp.float32, -s, s)
        bk = jax.random.uniform(ks[4], (EMBED,), jnp.float32, -s, s)
        Wv = jax.random.uniform(ks[5], (EMBED, EMBED), jnp.float32, -s, s)
        bv = jax.random.uniform(ks[6], (EMBED,), jnp.float32, -s, s)
        Wo = jax.random.uniform(ks[7], (EMBED, EMBED), jnp.float32, -s, s)
        bo = jax.random.uniform(ks[8], (EMBED,), jnp.float32, -s, s)
        return {'x': x, 'Wq': Wq, 'bq': bq, 'Wk': Wk, 'bk': bk, 'Wv': Wv, 'bv': bv, 'Wo': Wo, 'bo': bo}
    _L0_attn_in = _L0_attn_setup()

    def _L0_ffn_setup():
        import jax, jax.numpy as jnp
        import numpy as np
        HIDDEN_SIZE = 128
        NUM_EXPERTS = 8
        MOE_INTERMEDIATE_SIZE = 176
        NUM_EXPERTS_PER_TOK = 2
        SHARED_EXPERT_INTERMEDIATE_SIZE = 352
        B, T = (2, 128)
        W_SCALE = 0.02
        key = jax.random.key(seed)
        ks = jax.random.split(key, 8)
        H, E, I, SI = (HIDDEN_SIZE, NUM_EXPERTS, MOE_INTERMEDIATE_SIZE, SHARED_EXPERT_INTERMEDIATE_SIZE)
        return {'x': jax.random.normal(ks[0], (B, T, H), jnp.float32), 'gate_w': jax.random.normal(ks[1], (E, H), jnp.float32) * W_SCALE, 'experts_gate_up': jax.random.normal(ks[2], (E, 2 * I, H), jnp.float32) * W_SCALE, 'experts_down': jax.random.normal(ks[3], (E, H, I), jnp.float32) * W_SCALE, 'shared_gate_w': jax.random.normal(ks[4], (SI, H), jnp.float32) * W_SCALE, 'shared_up_w': jax.random.normal(ks[5], (SI, H), jnp.float32) * W_SCALE, 'shared_down_w': jax.random.normal(ks[6], (H, SI), jnp.float32) * W_SCALE, 'shared_expert_gate_w': jax.random.normal(ks[7], (1, H), jnp.float32) * W_SCALE}
    _L0_ffn_in = _L0_ffn_setup()

    def _L1_attn_setup():
        import jax, jax.numpy as jnp
        import numpy as np
        import math
        NUM_HEADS = 8
        EMB = 128
        HEAD_DIM = 128
        B, T = (1, 512)

        def sinusoidal_pe(T, d, dtype=jnp.float32):
            pos = jnp.arange(T, dtype=dtype)[:, None]
            inv_freq = jnp.exp(-math.log(10000.0) * jnp.arange(0, d, 2, dtype=dtype) / d)
            ang = pos * inv_freq[None, :]
            pe = jnp.zeros((T, d), dtype=dtype)
            pe = pe.at[:, 0::2].set(jnp.sin(ang))
            pe = pe.at[:, 1::2].set(jnp.cos(ang))
            return pe
        key = jax.random.key(seed)
        ks = jax.random.split(key, 6)
        s = lambda fan_in: 1.0 / math.sqrt(fan_in)
        x = jax.random.normal(ks[0], (B, T, EMB), dtype=jnp.float32)
        Wq = jax.random.normal(ks[1], (EMB, NUM_HEADS * HEAD_DIM), dtype=jnp.float32) * s(EMB)
        bq = jax.random.normal(ks[2], (NUM_HEADS * HEAD_DIM,), dtype=jnp.float32) * s(EMB)
        Wkv = jax.random.normal(ks[3], (EMB, 2 * HEAD_DIM), dtype=jnp.float32) * s(EMB)
        bkv = jax.random.normal(ks[4], (2 * HEAD_DIM,), dtype=jnp.float32) * s(EMB)
        Wo = jax.random.normal(ks[5], (NUM_HEADS * HEAD_DIM, EMB), dtype=jnp.float32) * s(NUM_HEADS * HEAD_DIM)
        return {'x': x, 'Wq': Wq, 'bq': bq, 'Wkv': Wkv, 'bkv': bkv, 'Wo': Wo}
    _L1_attn_in = _L1_attn_setup()

    def _L1_ffn_setup():
        import jax, jax.numpy as jnp
        import numpy as np
        NUM_EXPERTS = 8
        IN_FEATURES = 128
        HIDDEN_FEATURES = 512
        GATE_DIM = 16
        EPS = 0.0001
        key = jax.random.key(seed)
        ks = jax.random.split(key, 7)
        hidden_states = jax.random.normal(ks[0], (1, 256, IN_FEATURES), dtype=jnp.float32)
        wg_red = jax.random.normal(ks[1], (GATE_DIM, IN_FEATURES), dtype=jnp.float32) * 0.02
        wg = jax.random.normal(ks[2], (NUM_EXPERTS, GATE_DIM), dtype=jnp.float32)
        w1 = jax.random.uniform(ks[3], (NUM_EXPERTS, IN_FEATURES, HIDDEN_FEATURES), dtype=jnp.float32)
        b1 = jax.random.uniform(ks[4], (NUM_EXPERTS, HIDDEN_FEATURES), dtype=jnp.float32)
        w2 = jax.random.uniform(ks[5], (NUM_EXPERTS, HIDDEN_FEATURES, IN_FEATURES), dtype=jnp.float32)
        b2 = jax.random.uniform(ks[6], (NUM_EXPERTS, IN_FEATURES), dtype=jnp.float32)
        return {'hidden_states': hidden_states, 'wg_red': wg_red, 'wg': wg, 'w1': w1, 'b1': b1, 'w2': w2, 'b2': b2}
    _L1_ffn_in = _L1_ffn_setup()
    _d = {'L0_attn_x': _L0_attn_in['x'], 'L0_attn_Wq': _L0_attn_in['Wq'], 'L0_attn_bq': _L0_attn_in['bq'], 'L0_attn_Wk': _L0_attn_in['Wk'], 'L0_attn_bk': _L0_attn_in['bk'], 'L0_attn_Wv': _L0_attn_in['Wv'], 'L0_attn_bv': _L0_attn_in['bv'], 'L0_attn_Wo': _L0_attn_in['Wo'], 'L0_attn_bo': _L0_attn_in['bo'], 'L0_ffn_gate_w': _L0_ffn_in['gate_w'], 'L0_ffn_experts_gate_up': _L0_ffn_in['experts_gate_up'], 'L0_ffn_experts_down': _L0_ffn_in['experts_down'], 'L0_ffn_shared_gate_w': _L0_ffn_in['shared_gate_w'], 'L0_ffn_shared_up_w': _L0_ffn_in['shared_up_w'], 'L0_ffn_shared_down_w': _L0_ffn_in['shared_down_w'], 'L0_ffn_shared_expert_gate_w': _L0_ffn_in['shared_expert_gate_w'], 'L1_attn_Wq': _L1_attn_in['Wq'], 'L1_attn_bq': _L1_attn_in['bq'], 'L1_attn_Wkv': _L1_attn_in['Wkv'], 'L1_attn_bkv': _L1_attn_in['bkv'], 'L1_attn_Wo': _L1_attn_in['Wo'], 'L1_ffn_wg_red': _L1_ffn_in['wg_red'], 'L1_ffn_wg': _L1_ffn_in['wg'], 'L1_ffn_w1': _L1_ffn_in['w1'], 'L1_ffn_b1': _L1_ffn_in['b1'], 'L1_ffn_w2': _L1_ffn_in['w2'], 'L1_ffn_b2': _L1_ffn_in['b2']}
    _x0 = _d['L0_attn_x']
    _d['L0_attn_x'] = jax.random.normal(jax.random.fold_in(jax.random.key(seed), 1), (8, 256, 128), dtype=_x0.dtype)
    del _x0
    return _d

def reference(L0_attn_x, L0_attn_Wq, L0_attn_bq, L0_attn_Wk, L0_attn_bk, L0_attn_Wv, L0_attn_bv, L0_attn_Wo, L0_attn_bo, L0_ffn_gate_w, L0_ffn_experts_gate_up, L0_ffn_experts_down, L0_ffn_shared_gate_w, L0_ffn_shared_up_w, L0_ffn_shared_down_w, L0_ffn_shared_expert_gate_w, L1_attn_Wq, L1_attn_bq, L1_attn_Wkv, L1_attn_bkv, L1_attn_Wo, L1_ffn_wg_red, L1_ffn_wg, L1_ffn_w1, L1_ffn_b1, L1_ffn_w2, L1_ffn_b2):

    def _L0_attn_ref(x, Wq, bq, Wk, bk, Wv, bv, Wo, bo):
        import jax, jax.numpy as jnp
        import numpy as np
        EMBED = 128
        HEADS = 16
        HEAD_DIM = EMBED // HEADS
        B, S, E = x.shape
        H, D = (HEADS, HEAD_DIM)

        def proj(W, b):
            return (x @ W + b).reshape(B, S, H, D).transpose(0, 2, 1, 3)
        q, k, v = (proj(Wq, bq), proj(Wk, bk), proj(Wv, bv))
        scores = jnp.einsum('bhsd,bhtd->bhst', q, k) / jnp.sqrt(jnp.float32(D))
        attn = jax.nn.softmax(scores, axis=-1)
        out = jnp.einsum('bhst,bhtd->bhsd', attn, v)
        out = out.transpose(0, 2, 1, 3).reshape(B, S, E)
        return out @ Wo + bo

    def _L0_ffn_ref(x, gate_w, experts_gate_up, experts_down, shared_gate_w, shared_up_w, shared_down_w, shared_expert_gate_w):
        import jax, jax.numpy as jnp
        import numpy as np
        HIDDEN_SIZE = 128
        NUM_EXPERTS = 8
        MOE_INTERMEDIATE_SIZE = 176
        NUM_EXPERTS_PER_TOK = 2
        SHARED_EXPERT_INTERMEDIATE_SIZE = 352
        B, T = (2, 128)
        W_SCALE = 0.02
        Bx, Tx, H = x.shape
        E = gate_w.shape[0]
        I = experts_down.shape[2]
        x_flat = x.reshape(Bx * Tx, H)
        logits = x_flat @ gate_w.T
        scores = jax.nn.softmax(logits, axis=-1)
        _, topk_ids = jax.lax.top_k(scores, NUM_EXPERTS_PER_TOK)
        in_topk = jax.nn.one_hot(topk_ids, E, dtype=x.dtype).sum(axis=1)
        w = scores * in_topk
        gu = jnp.einsum('nh,eih->nei', x_flat, experts_gate_up)
        g, u = (gu[..., :I], gu[..., I:])
        h = jax.nn.silu(g) * u
        expert_out = jnp.einsum('nei,ehi->neh', h, experts_down)
        out = jnp.einsum('neh,ne->nh', expert_out, w)
        shared = jax.nn.silu(x_flat @ shared_gate_w.T) * (x_flat @ shared_up_w.T) @ shared_down_w.T
        shared_weight = jax.nn.sigmoid(x_flat @ shared_expert_gate_w.T)
        out = out + shared_weight * shared
        return out.reshape(Bx, Tx, H)

    def _L1_attn_ref(x, Wq, bq, Wkv, bkv, Wo):
        import jax, jax.numpy as jnp
        import numpy as np
        import math
        NUM_HEADS = 8
        EMB = 128
        HEAD_DIM = 128
        B, T = (1, 512)

        def sinusoidal_pe(T, d, dtype=jnp.float32):
            pos = jnp.arange(T, dtype=dtype)[:, None]
            inv_freq = jnp.exp(-math.log(10000.0) * jnp.arange(0, d, 2, dtype=dtype) / d)
            ang = pos * inv_freq[None, :]
            pe = jnp.zeros((T, d), dtype=dtype)
            pe = pe.at[:, 0::2].set(jnp.sin(ang))
            pe = pe.at[:, 1::2].set(jnp.cos(ang))
            return pe
        Bsz, Tlen, E = x.shape
        q = (x @ Wq + bq).reshape(Bsz, Tlen, NUM_HEADS, HEAD_DIM)
        kv = x @ Wkv + bkv
        k, v = (kv[..., :HEAD_DIM], kv[..., HEAD_DIM:])
        q = jnp.transpose(q, (0, 2, 1, 3))
        pe = sinusoidal_pe(Tlen, HEAD_DIM, x.dtype)
        q = q + pe[None, None, :, :]
        k = k + pe[None, :, :]
        scale = 1.0 / math.sqrt(HEAD_DIM)
        scores = jnp.einsum('bhqd,bkd->bhqk', q, k) * scale
        causal = jnp.tril(jnp.ones((Tlen, Tlen), dtype=bool))
        scores = jnp.where(causal[None, None, :, :], scores, jnp.finfo(scores.dtype).min)
        probs = jax.nn.softmax(scores, axis=-1)
        attn = jnp.einsum('bhqk,bkd->bhqd', probs, v)
        out = jnp.transpose(attn, (0, 2, 1, 3)).reshape(Bsz, Tlen, NUM_HEADS * HEAD_DIM)
        return out @ Wo

    def _L1_ffn_ref(hidden_states, wg_red, wg, w1, b1, w2, b2):
        import jax, jax.numpy as jnp
        import numpy as np
        NUM_EXPERTS = 8
        IN_FEATURES = 128
        HIDDEN_FEATURES = 512
        GATE_DIM = 16
        EPS = 0.0001
        b, t, c = hidden_states.shape
        x = hidden_states.reshape(-1, c)
        xr = x @ wg_red.T
        wg_unit = wg / jnp.maximum(jnp.linalg.norm(wg, axis=1, keepdims=True), EPS)
        logits = xr @ wg_unit.T
        gates = jax.nn.softmax(logits, axis=1)
        indices_s = jnp.argmax(gates, axis=1)
        scores = jnp.max(gates, axis=1)
        E = wg.shape[0]
        out = jnp.zeros_like(x)
        for e in range(E):
            mask = (indices_s == e).astype(x.dtype)[:, None]
            h = jax.nn.gelu(x @ w1[e] + b1[e], approximate=False)
            out = out + mask * (h @ w2[e] + b2[e])
        out = out * scores[:, None]
        return out.reshape(b, t, c)
    x = L0_attn_x
    xn = _layernorm(x, axis=-1)
    x = x + _L0_attn_ref(xn, L0_attn_Wq, L0_attn_bq, L0_attn_Wk, L0_attn_bk, L0_attn_Wv, L0_attn_bv, L0_attn_Wo, L0_attn_bo) + _L0_ffn_ref(xn, L0_ffn_gate_w, L0_ffn_experts_gate_up, L0_ffn_experts_down, L0_ffn_shared_gate_w, L0_ffn_shared_up_w, L0_ffn_shared_down_w, L0_ffn_shared_expert_gate_w)
    xn = _layernorm(x, axis=-1)
    x = x + _L1_attn_ref(xn, L1_attn_Wq, L1_attn_bq, L1_attn_Wkv, L1_attn_bkv, L1_attn_Wo) + _L1_ffn_ref(xn, L1_ffn_wg_red, L1_ffn_wg, L1_ffn_w1, L1_ffn_b1, L1_ffn_w2, L1_ffn_b2)
    return x

_drawn_inputs = setup_inputs


def setup_inputs(seed=0):
    import zlib

    import numpy as np

    out = dict(_drawn_inputs(seed))
    spreads = {}
    factors = {'L0_attn_Wq': 6.35,
     'L0_attn_bq': 8.0,
     'L0_attn_Wk': 6.14,
     'L0_attn_bk': 8.0,
     'L0_attn_Wv': 4.221,
     'L0_attn_bv': 2.757,
     'L0_attn_Wo': 3.345,
     'L0_attn_bo': 3.145,
     'L0_ffn_gate_w': 8.0,
     'L0_ffn_experts_gate_up': 8.0,
     'L0_ffn_experts_down': 8.0,
     'L0_ffn_shared_gate_w': 8.0,
     'L0_ffn_shared_up_w': 8.0,
     'L0_ffn_shared_down_w': 8.0,
     'L0_ffn_shared_expert_gate_w': 8.0,
     'L1_attn_Wq': 8.0,
     'L1_attn_bq': 8.0,
     'L1_attn_Wkv': 8.0,
     'L1_attn_bkv': 8.0,
     'L1_attn_Wo': 8.0,
     'L1_ffn_b1': 8.0,
     'L1_ffn_b2': 8.0}
    for name, (base, spread) in spreads.items():
        noise = np.random.default_rng([zlib.crc32(name.encode()), seed]).standard_normal(out[name].shape)
        drawn = base * np.exp(spread * noise) if base else spread * noise
        out[name] = jnp.asarray(drawn.astype(out[name].dtype))
    for name, factor in factors.items():
        out[name] = (out[name] * factor).astype(out[name].dtype)
    return out
```

```python
from contextlib import ExitStack

import concourse.bass as bass
from concourse import mybir

ALU = mybir.AluOpType
ACT = mybir.ActivationFunctionType
AX = mybir.AxisListType
F32 = mybir.dt.float32
BF16 = mybir.dt.bfloat16
F16 = mybir.dt.float16
U32 = mybir.dt.uint32
I32 = mybir.dt.int32

P = 128
B, S = 8, 256
C = S // P
NT = B * C
NTOK = NT * P
EPS_LN = 1e-5
E = 8
CREDIT = 18

H0, D0 = 16, 8
I0 = 176
SI = 352
SJ = 3
K0 = 2
T0 = 40
QPARTS = (0, 0, 1, 0, 1, 2)
KPARTS = (0, 1, 0, 2, 1, 0)
PAIRS = tuple(tuple(zip([g for g, p in enumerate(QPARTS) if p == part], [g for g, p in enumerate(KPARTS) if p == part]))
              for part in range(3))
NP0 = len(QPARTS)
MROW = NP0 * D0
SROW = MROW + 3
VC = D0 + 1
SCALE0 = float(D0) ** -0.5

H1 = 8
HID1 = 512
T1 = 24
SCALE1 = float(P) ** -0.5
GD = 16
EPS_NORM = 1e-4
NEG = -3.0e38

DUMP = K0 * NTOK
ROW = P + 2


def const_layout():
    at, out = 0, {}
    for name, n in (("ident", P), ("before", P), ("tile_before", P), ("same_expert", E), ("first", E),
                    ("steps", NT), ("tiles", T0), ("token", K0 * NT), ("dump", T0), ("mask", P), ("pe", S)):
        out[name] = (at, at + n)
        at += n
    return out, at


def build(nc, a, out):
    ctx = ExitStack()
    with ctx:
        sems = []

        def sem(name, software_dma=False):
            s = ctx.enter_context(nc.semaphore(name))
            if not software_dma:
                sems.append(s)
            return s

        def sb(name, shape, dt=F32):
            return ctx.enter_context(nc.sbuf_tensor("sb_" + name, shape, dt))

        def wait(eng, s, count):
            if not isinstance(count, int) or count > 0:
                eng.wait_ge(s, count + CREDIT)

        def wait_dma(eng, s, count):
            if not isinstance(count, int) or count > 0:
                eng.wait_ge(s, count * 16 + CREDIT)

        psum = ctx.enter_context(nc.psum_tensor("psum", [P, 8, 512], F32))
        bank = [psum[:, i, :] for i in range(8)]

        def wait_scatter(eng, s, count):
            if not isinstance(count, int) or count > 0:
                eng.wait_ge(s, count * 16)

        def at(i, n):
            return slice(i, i + n) if isinstance(i, int) else bass.ds(i, n)

        cols, ncols = const_layout()
        const = sb("const", [P, ncols])

        def cst(name):
            return const[:, cols[name][0]:cols[name][1]]

        ident = cst("ident")
        x_sb = sb("x_sb", [P, NT, P])
        xr = sb("xr", [P, NT, ROW])
        side = sb("side", [P, NT, P])
        xnT1 = sb("xnT1", [P, NTOK])
        xn = [sb(f"xn{k}", [P, C, P]) for k in range(2)]
        xT = [sb(f"xT{k}", [P, S]) for k in range(2)]
        st = sb("st", [P, NT, 6])
        mv = sb("mv", [P, NT, 2])
        rstd = sb("rstd", [P, NT])
        rtmp = sb("rtmp", [P, NT])
        rvar = sb("rvar", [P, NT])
        lg = sb("lg", [P, NT, E + 1])
        ident16 = sb("ident16", [P, P], BF16)
        before16 = sb("before16", [P, P], BF16)
        tile_before16 = sb("tile_before16", [P, P], BF16)
        same16 = sb("same16", [P, E], BF16)
        ones16 = sb("ones16", [P, P], BF16)
        mask16 = sb("mask16", [P, P], BF16)

        w_qkvo = sb("w_qkvo", [P, 4, P])
        b_qk = sb("b_qk", [P, 2])
        bv_row = sb("bv_row", [P, P])
        bo_row = sb("bo_row", [P, P])
        w_gate0 = sb("w_gate0", [P, E + 1])
        w_sgu = sb("w_sgu", [P, 2, SJ, P])
        w_sd = sb("w_sd", [P, SJ, P])
        w_gu0 = sb("w_gu0", [P, E, 2 * I0])
        w_dn0 = sb("w_dn0", [P, E, 2, P])
        w_q1 = sb("w_q1", [P, H1 * P])
        b_q1 = sb("b_q1", [P, H1])
        w_kv1 = sb("w_kv1", [P, 2 * P])
        b_kv1 = sb("b_kv1", [P, 2])
        w_o1 = sb("w_o1", [P, H1, P])
        w_red1 = sb("w_red1", [P, GD])
        wg1 = sb("wg1", [E, GD])
        wg1s = sb("wg1s", [E, GD])
        wgn = sb("wgn", [E, 3])
        wgT = sb("wgT", [GD, E])

        HG = 4

        class Region:

            def __init__(self, name, words):
                self.memory, self.words, self.used = sb(name, [P, words]), words, {}

            def take(self, user, shape, dt=F32, partitions=P):
                words = 1
                for n in shape:
                    words *= n
                words = words * mybir.dt.size(dt) // 4
                at = self.used.get(user, 0)
                self.used[user] = at + words
                assert at + words <= self.words, (user, at + words)
                flat = self.memory[0:partitions, at:at + words]
                if dt != F32:
                    flat = flat.bitcast(dt)
                names = "abcd"[:len(shape)]
                return flat.rearrange(f"p ({' '.join(names)}) -> p {' '.join(names)}", **dict(zip(names, shape)))

        arena = Region("arena", 16384)
        bench = Region("bench", 8960)
        region = arena.take
        v0 = bench.take("prepare", [NT, H0, VC])

        stQ = [region("attention", [H0, S], BF16) for k in range(2)]
        stK = [region("attention", [H0, S], BF16) for k in range(2)]

        w_up1 = region("weights", [E, HID1])
        w_dn1 = region("weights", [4, E, P])
        b_up1 = region("weights", [E, HID1])
        b_dn1 = region("weights", [E, P])

        qk_scr = nc.dram_tensor("qk_scr", [B, 2, SROW, H0 * S], BF16, kind="Internal").ap()
        slots = [nc.dram_tensor(f"slots{n}", [t * P, ROW], F32, kind="Internal").ap() for n, t in ((0, T0), (1, T1))]
        ys = [nc.dram_tensor(f"ys{n}", [DUMP + T0 * P, P], F32, kind="Internal").ap() for n in range(2)]

        parts = {n: [] for n in ("sync", "scalar", "vector", "gpsimd", "tensor")}

        def on(engine):
            def add(f):
                parts[engine].append(f)
                return f
            return add

        class Chain:

            def __init__(self, name):
                self.sem, self.base, self.n = sem(name), 0, 0

            def inc(self, ins):
                ins.then_inc(self.sem, 1)
                self.n += 1
                return ins

            def sync(self, eng):
                wait(eng, self.sem, self.base + self.n)

            def link(self, eng, ins):
                self.inc(ins)
                self.sync(eng)

            def loop(self, eng, count, k, body):
                start = self.base + self.n
                with eng.Fori(0, count) as i:
                    self.base, self.n = start + i * k, 0
                    body(i)
                    assert self.n == k, (self.n, k)
                self.base, self.n = start + count * k, 0

        dve = Chain("c_dve")
        pool = Chain("c_pool")
        act = Chain("c_act")

        def pairs(eng, chain, k, step, peel=0, first=True):
            for b in range(2 * peel if first else 0):
                step(b, b % 2, b // 2)

            def body(i):
                half = i + peel
                step(half * 2, 0, half)
                step(half * 2 + 1, 1, half)
            if chain is None:
                with eng.Fori(0, B // 2 - 1 - peel) as i:
                    body(i)
            else:
                chain.loop(eng, B // 2 - 1 - peel, k, body)
            step(B - 2, 0, B // 2 - 1)
            step(B - 1, 1, B // 2 - 1)

        def is_last(b):
            return isinstance(b, int) and b == B - 1

        s_x = [sem(f"s_xin{n}") for n in range(4)]
        s_wg1 = sem("s_wg1")
        s_const = sem("s_const")
        s_w0 = sem("s_w0")
        s_shared = sem("s_shared")
        s_pads = sem("s_pads")
        s_exp0 = sem("s_exp0")
        s_w1 = sem("s_w1")
        s_exp1 = sem("s_exp1")

        def row_bcast(v):
            return v.rearrange("(o n) -> o n", o=1).broadcast_to([P, v.shape[0]])

        @on("sync")
        def _(sp):
            sp.dma_start(wg1[:, :], a["wg1"]).then_inc(s_wg1, 16)
            for n in range(4):
                sp.dma_start(x_sb[:, 4 * n:4 * n + 4, :], a["x"].rearrange("(i p) d -> p i d", p=P)[:, 4 * n:4 * n + 4, :]).then_inc(s_x[n], 16)
            sp.dma_start(const[:, :], a["const"]).then_inc(s_const, 16)
            for n, name in enumerate(("Wq0", "Wk0", "Wv0", "Wo0")):
                sp.dma_start(w_qkvo[:, n, :], a[name]).then_inc(s_w0, 16)
            for n, name in enumerate(("bq0", "bk0")):
                sp.dma_start(b_qk[:, n:n + 1], a[name].rearrange("(p o) -> p o", o=1)).then_inc(s_w0, 16)
            sp.dma_start(bv_row[:, :], row_bcast(a["bv0"])).then_inc(s_w0, 16)
            sp.dma_start(bo_row[:, :], row_bcast(a["bo0"])).then_inc(s_w0, 16)
            sp.dma_start(w_gate0[:, :], a["gate0"]).then_inc(s_w0, 16)
            wait(sp, s_pads, 1)
            for n, name in enumerate(("sgate", "sup")):
                sp.dma_start(w_sgu[:, n, :, :].rearrange("p j n -> p (j n)")[:, 0:SI], a[name]).then_inc(s_shared, 16)
            sp.dma_start(w_sd[:, 0:2, :], a["sdown"][0:2 * P, :].rearrange("(j p) n -> p j n", p=P)).then_inc(s_shared, 16)
            sp.dma_start(w_sd[0:SI - 2 * P, 2, :], a["sdown"][2 * P:SI, :]).then_inc(s_shared, 16)
        N_W0, N_SHARED, N_EXP0 = 9, 4, 3

        N_W1, N_EXP1 = 6, 4 * E

        s_var = sem("s_var")
        s_std = sem("s_std")

        def layer_stats(n, arrive):
            @on("vector")
            def _(v):
                for piece in range(4):
                    arrive(v, piece)
                    rows = range(piece * NT // 4, (piece + 1) * NT // 4)
                    for i in rows:
                        dve.inc(v.bn_stats(st[:, i, :], x_sb[:, i, :]))
                    dve.sync(v)
                    for i in rows:
                        dve.inc(v.bn_aggr(mv[:, i, :], st[:, i, :]))
                dve.sync(v)
                v.tensor_scalar(rvar[:, :], mv[:, :, 1], EPS_LN, None, ALU.add).then_inc(s_var, 1)
                wait(v, s_std, n + 1)
                dve.link(v, v.reciprocal(rstd[:, :], rtmp[:, :]))
                wait(v, s_var, n + 1)
                dve.link(v, v.tensor_tensor(rtmp[:, :], rvar[:, :], rstd[:, :], ALU.mult))
                dve.link(v, v.tensor_tensor(rtmp[:, :], rtmp[:, :], rstd[:, :], ALU.mult))
                dve.link(v, v.tensor_scalar(rtmp[:, :], rtmp[:, :], -0.5, 1.5, ALU.mult, ALU.add))
                dve.link(v, v.tensor_tensor(rstd[:, :], rstd[:, :], rtmp[:, :], ALU.mult))

            @on("scalar")
            def _(s):
                wait(s, s_var, n + 1)
                s.activation(rtmp[:, :], rvar[:, :], ACT.Sqrt).then_inc(s_std, 1)

        def normalise(v, b, k, dst_free):
            for c in range(C):
                i = b * C + c
                ins = v.tensor_scalar(xn[k][:, c, :], x_sb[:, i, :], mv[:, i, 0:1], rstd[:, at(i, 1)],
                                      ALU.subtract, ALU.mult)
            ins.then_inc(dst_free, 1)

        s_c16 = sem("s_c16")
        s_slot_init = sem("s_slot_init")
        s_pad_rows = sem("s_pad_rows")
        s_fixed_out = sem("s_fixed_out")
        s_fixed = sem("s_fixed")
        s_stack0 = sem("s_stack0")
        arena.take("padding", [2 * 2 * H0 * S // 2])
        pad_rows = arena.take("padding", [T0, ROW])
        FW = 3 * H0 * S // P
        fixed = [bench.take("prepare", [FW], BF16) for z in range(2)]

        @on("gpsimd")
        def _(g):
            pool.inc(g.memset(w_sgu[:, :, 2, :], 0.0))
            g.memset(w_sd[:, 2, :], 0.0)
            pool.inc(g.memset(w_dn0[:, :, 1, :], 0.0))
            pool.sync(g)
            g.memset(ones16[:, :], 1.0).then_inc(s_pads, 1)
            g.memset(fixed[0][:, :], 0.0).then_inc(s_fixed, 1)
            g.memset(fixed[1][:, :], -1.0).then_inc(s_fixed, 1)
            wait_dma(g, s_const, 1)
            g.tensor_copy(before16[:, :], cst("before"))
            g.tensor_copy(tile_before16[:, :], cst("tile_before"))
            g.tensor_copy(same16[:, :], cst("same_expert"))
            g.tensor_copy(ident16[:, :], ident)
            g.tensor_copy(mask16[:, :], cst("mask")).then_inc(s_c16, 1)
            g.memset(te[:, :].bitcast(F32), 0.0).then_inc(s_c16, 1)
            g.memset(v0[:, :, :, :], 1.0).then_inc(s_c16, 1)
            for k in range(2):
                g.memset(stQ[k][:, :, :].rearrange("p h s -> p (h s)").bitcast(F32), 0.0).then_inc(s_stack0, 1)
                g.memset(stK[k][:, :, :].rearrange("p h s -> p (h s)").bitcast(F32), 0.0).then_inc(s_stack0, 1)
            pool.link(g, g.memset(pad_rows[:, :, :], 0.0))
            g.tensor_copy(pad_rows[:, :, ROW - 1], cst("dump")).then_inc(s_pad_rows, 1)

        @on("sync")
        def _(sp):
            wait(sp, s_fixed, 2)
            for z in range(2):
                rows = qk_scr[:, z, MROW:SROW, :].rearrange("b t n -> b (t n)").rearrange("b (p n) -> p b n", p=P)
                sp.dma_start(rows, fixed[z][:, :].unsqueeze(1).broadcast_to([P, B, FW])).then_inc(s_fixed_out, 16)
        N_INIT = 2

        s_xn = sem("s_xn")
        s_xr = sem("s_xr")
        s_tx = sem("s_tx")
        s_xT = sem("s_xT")
        s_qk = sem("s_qk")
        s_q32 = sem("s_q32")
        s_qh = sem("s_qh")
        s_r1 = sem("s_r1")
        s_qm = sem("s_qm")
        s_ql = sem("s_ql")
        s_qst = [sem(f"s_qst{k}") for k in range(2)]
        s_v = sem("s_v")
        s_vp = sem("s_vp")
        s_wg = sem("s_wg")
        s_wgt = sem("s_wgt")
        s_g = sem("s_g")
        s_sg = sem("s_sg")
        s_hs = sem("s_hs")
        s_dn = sem("s_dn")
        s_sh = sem("s_sh")
        B_T, B_QK, B_V, B_D = bank[0], bank[1], bank[2], bank[3]
        B_G = bank[4:7]
        qk32 = bench.take("prepare", [2 * S])
        qkr = bench.take("prepare", [2 * S])
        qp = [bench.take("prepare", [3, 2 * S], BF16) for k in range(2)]
        silu_s = [bench.take("prepare", [S]) for j in range(SJ)]
        hid_s = [bench.take("prepare", [SJ, S]) for k in range(2)]

        @on("vector")
        def _(v):
            wait_dma(v, s_wg1, 1)
            dve.link(v, v.tensor_tensor(wg1s[:, :], wg1[:, :], wg1[:, :], ALU.mult))
            dve.link(v, v.tensor_reduce(wgn[:, 0:1], wg1s[:, :], AX.X, ALU.add))
            v.tensor_scalar(wgn[:, 0:1], wgn[:, 0:1], EPS_NORM * EPS_NORM, None, ALU.max).then_inc(s_wg, 1)
            wait(v, s_wg, 2)
            dve.link(v, v.reciprocal(wgn[:, 1:2], wgn[:, 1:2]))
            for a_, b_ in ((0, 1), (2, 1)):
                dve.link(v, v.tensor_tensor(wgn[:, 2:3], wgn[:, a_:a_ + 1], wgn[:, b_:b_ + 1], ALU.mult))
            dve.link(v, v.tensor_scalar(wgn[:, 2:3], wgn[:, 2:3], -0.5, 1.5, ALU.mult, ALU.add))
            dve.link(v, v.tensor_tensor(wgn[:, 1:2], wgn[:, 1:2], wgn[:, 2:3], ALU.mult))
            v.tensor_scalar(wg1s[:, :], wg1[:, :], wgn[:, 1:2], None, ALU.mult).then_inc(s_wg, 1)

        @on("scalar")
        def _(s):
            wait(s, s_wg, 1)
            s.activation(wgn[:, 1:2], wgn[:, 0:1], ACT.Sqrt).then_inc(s_wg, 1)


        layer_stats(0, lambda v, piece: wait_dma(v, s_x[piece], 1))

        @on("vector")
        def _(v):
            wait(v, s_wgt, 1)
            v.tensor_copy(wgT[:, :], B_D[0:GD, 0:E]).then_inc(s_wg, 1)
            wait(v, s_c16, 3)
            wait_dma(v, s_w0, N_W0)
            normalise(v, 0, 0, s_xn)

            def step(b, k, half):
                if not is_last(b):
                    wait(v, s_tx, b)
                    wait(v, s_xr, b)
                    normalise(v, b + 1, 1 - k, s_xn)
                wait(v, s_qk, b + 1)
                wait(v, s_ql, b)
                for n in range(2):
                    ins = v.tensor_scalar(qk32[:, n * S:(n + 1) * S], B_QK[:, n * S:(n + 1) * S], b_qk[:, n:n + 1],
                                          None, ALU.add)
                ins.then_inc(s_q32, 1)
                wait(v, s_v, b + 1)
                tiles = at(b * C, C)
                for c in range(C):
                    v.tensor_tensor(v0[:, b * C + c, :, 0:D0], B_V[:, c * P:(c + 1) * P].rearrange("p (h d) -> p h d", d=D0),
                                    bv_row[:, :].rearrange("p (h d) -> p h d", d=D0), ALU.add)
                v.tensor_copy(lg[:, tiles, :],
                              B_V[:, S:S + C * (E + 1)].rearrange("p (c e) -> p c e", c=C)).then_inc(s_vp, 1)
                hidden(v, b, k, 0)
                wait(v, s_qh, b + 1)
                v.tensor_tensor(qkr[:, :], qk32[:, :], qp[k][:, 0, :], ALU.subtract).then_inc(s_r1, 1)
                hidden(v, b, k, 1)
                wait(v, s_qm, b + 1)
                v.tensor_tensor(qp[k][:, 2, :], qkr[:, :], qp[k][:, 1, :], ALU.subtract).then_inc(s_ql, 1)
                if not (isinstance(b, int) and b == 0):
                    shared(b - 1)
                hidden(v, b, k, 2)

            def shared(b):
                wait(v, s_dn, b + 1)
                v.tensor_copy(side[:, at(b * C, C), :], B_D[:, 0:S].rearrange("p (c n) -> p c n", c=C)).then_inc(s_sh, 1)

            def hidden(v, b, k, j):
                if j == 0:
                    wait(v, s_dn, b - 1)
                wait(v, s_sg, b * SJ + j + 1)
                v.tensor_tensor(hid_s[k][:, j, :], silu_s[j][:, :], B_G[j][:, S:2 * S], ALU.mult).then_inc(s_hs, 1)

            pairs(v, None, 0, step, peel=1)
            shared(B - 1)

        @on("gpsimd")
        def _(g):
            def step(b, k, half):
                wait(g, s_xn, b + 1)
                tiles = at(b * C, C)
                g.tensor_copy(xr[:, tiles, 0:P], xn[k][:, :, :]).then_inc(s_xr, 1)
            pairs(g, None, 0, step)

        @on("scalar")
        def _(s):
            def evacuate_xT(b, k):
                wait(s, s_tx, b + 1)
                wait(s, s_g, (b - 1) * SJ)
                s.copy(xT[k][:, :], B_T[:, 0:S]).then_inc(s_xT, 1)
            evacuate_xT(0, 0)

            def silu(b, k, j):
                wait(s, s_g, b * SJ + j + 1)
                wait(s, s_hs, (b - 1) * SJ + j + 1)
                s.activation(silu_s[j][:, :], B_G[j][:, 0:S], ACT.Silu).then_inc(s_sg, 1)

            def step(b, k, half):
                wait(s, s_q32, b + 1)
                wait_dma(s, s_qst[k], half * NP0)
                s.copy(qp[k][:, 0, :], qk32[:, :]).then_inc(s_qh, 1)
                silu(b, k, 0)
                if not is_last(b):
                    evacuate_xT(b + 1, 1 - k)
                wait(s, s_r1, b + 1)
                s.copy(qp[k][:, 1, :], qkr[:, :]).then_inc(s_qm, 1)
                silu(b, k, 1)
                silu(b, k, 2)
            pairs(s, None, 0, step)

        @on("tensor")
        def _(t):
            wait_dma(t, s_const, 1)
            wait(t, s_wg, 3)
            t.transpose(B_D[0:GD, 0:E], wg1s[:, :], ident[0:E, 0:E]).then_inc(s_wgt, 1)

            def transpose_x(b, k):
                wait(t, s_xn, b + 1)
                wait(t, s_xT, b)
                for c in range(C):
                    mm = t.transpose(B_T[:, c * P:(c + 1) * P], xn[k][:, c, :], ident)
                mm.then_inc(s_tx, 1)
            transpose_x(0, 0)
            wait_dma(t, s_w0, N_W0)
            wait_dma(t, s_shared, N_SHARED)

            def step(b, k, half):
                wait(t, s_xT, b + 1)
                wait(t, s_q32, b)
                for n in range(2):
                    mm = t.matmul(B_QK[:, n * S:(n + 1) * S], w_qkvo[:, n, :], xT[k][:, :], start=True, stop=True)
                mm.then_inc(s_qk, 1)
                wait(t, s_vp, b)
                for c in range(C):
                    x_c = xT[k][:, c * P:(c + 1) * P]
                    t.matmul(B_V[:, c * P:(c + 1) * P], x_c, w_qkvo[:, 2, :], start=True, stop=True)
                    mm = t.matmul(B_V[:, S + c * (E + 1):S + (c + 1) * (E + 1)], x_c, w_gate0[:, :], start=True, stop=True)
                mm.then_inc(s_v, 1)
                gate_up(b, k, 0)
                if not is_last(b):
                    transpose_x(b + 1, 1 - k)
                gate_up(b, k, 1)
                if not (isinstance(b, int) and b == 0):
                    down(b - 1, 1 - k)
                gate_up(b, k, 2)

            def gate_up(b, k, j):
                wait(t, s_hs, (b - 1) * SJ + j + 1)
                for u in range(2):
                    mm = t.matmul(B_G[j][:, u * S:(u + 1) * S], w_sgu[:, u, j, :], xT[k][:, :], start=True, stop=True)
                mm.then_inc(s_g, 1)

            def down(b, k):
                wait(t, s_hs, (b + 1) * SJ)
                wait(t, s_sh, b)
                for c in range(C):
                    for j in range(SJ):
                        mm = t.matmul(B_D[:, c * P:(c + 1) * P], hid_s[k][:, j, c * P:(c + 1) * P], w_sd[:, j, :],
                                      start=(j == 0), stop=(j == SJ - 1))
                mm.then_inc(s_dn, 1)
            pairs(t, None, 0, step, peel=1)
            down(B - 1, 1)

        @on("sync")
        def _(sp):
            def step(b, k, half):
                for part, ready in enumerate((s_qh, s_qm, s_ql)):
                    wait(sp, ready, b + 1)
                    for gq, gk in PAIRS[part]:
                        place = qk_scr[b, 0, gq * D0:(gq + 1) * D0, :].rearrange("d (h s) -> (d h) s", h=H0)
                        both = bass.AP(tensor=place.tensor, offset=place.offset,
                                       ap=[place.ap[0], [(SROW + (gk - gq) * D0) * H0 * S, 2], place.ap[1]])
                        sp.dma_start(both, qp[k][:, part, :].rearrange("p (z s) -> p z s", z=2)).then_inc(s_qst[k], 16)
            pairs(sp, None, 0, step)

        def late_loads(sp):
            wait(sp, s_pad_rows, 1)
            for dst, t in ((slots[0], T0), (slots[1], T1)):
                sp.dma_start(dst.rearrange("(p t) r -> p (t r)", p=P),
                             pad_rows[:, 0:t, :].rearrange("p t r -> p (t r)")).then_inc(s_slot_init, 16)
            sp.dma_start(w_gu0[:, :, :], a["gu0"]).then_inc(s_exp0, 16)
            sp.dma_start(w_dn0[:, :, 0, :], a["down0"][:, 0:P, :].rearrange("e i n -> i e n")).then_inc(s_exp0, 16)
            sp.dma_start(w_dn0[0:I0 - P, :, 1, :], a["down0"][:, P:I0, :].rearrange("e i n -> i e n")).then_inc(s_exp0, 16)
            for dst, name in ((w_q1[:, :], "Wq1"), (w_kv1[:, :], "Wkv1"), (w_red1[:, :], "red1")):
                sp.dma_start(dst, a[name]).then_inc(s_w1, 16)
            with nc.allow_non_contiguous_dma(reason="a few bias columns"):
                sp.dma_start(b_q1[:, :], a["bq1"].rearrange("(h p) -> p h", p=P)).then_inc(s_w1, 16)
                sp.dma_start(b_kv1[:, :], a["bkv1"].rearrange("(h p) -> p h", p=P)).then_inc(s_w1, 16)
            sp.dma_start(w_o1[:, :, :], a["Wo1"].rearrange("(h p) n -> p h n", p=P)).then_inc(s_w1, 16)

        s_ex = sem("s_gate_exp")
        s_picked = sem("s_picked")
        s_ranked = sem("s_ranked")
        s_rank = sem("s_rank")
        s_route = sem("s_route")
        gates = sb("gates", [P, NT, E])
        g2 = sb("g2", [P, NT, E])
        pick = [sb(f"pick{n}", [P, NT, E]) for n in range(K0)]
        both16 = sb("both16", [P, NT, E], BF16)
        tot16 = sb("tot16", [P, P], BF16)
        gm = sb("gm", [P, NT])
        wk = sb("wk", [P, K0, NT])
        cand = sb("cand", [P, NT, E])
        counts = sb("counts", [P, E])
        ntile = sb("ntile", [P, E])
        cum = sb("cum", [P, E])
        start_ = sb("start_", [P, E])
        stepcmp = sb("stepcmp", [P, E, NT])
        tilecmp = sb("tilecmp", [P, T0, E - 1])
        tef = sb("tef", [P, T0])
        te = sb("te", [P, T0 + 8], I32)
        rank = sb("rank", [P, NT, E])
        posf = sb("posf", [P, NT])
        pos = sb("pos", [P, K0, NT], U32)
        sig = sb("sig", [P, NT])

        def routing(n, picks, T):
            B_TOT, B_RANK, B_CNT = bank[7][:, 0:P], bank[7][:, P:2 * P], bank[7][:, 2 * P:2 * P + E]

            def per_tile(ap):
                return ap.unsqueeze(2).broadcast_to([P, NT, E])

            def per_expert(ap):
                return ap.unsqueeze(1).broadcast_to([P, NT, E])

            def vector_steps(v):
                def link(ins):
                    dve.inc(ins)

                if n == 0:
                    wait(v, s_sh, B)
                logits = lg[:, :, 0:E]
                wait(v, s_vp if n == 0 else s_lg, B)
                link(v.tensor_reduce(gm[:, :], logits, AX.X, ALU.max))
                yield
                dve.sync(v)
                v.tensor_tensor(gates[:, :, :], logits, per_tile(gm[:, :]), ALU.subtract).then_inc(s_ex, 1)
                yield
                yield
                wait(v, s_ex, 2 + 2 * n)
                if n == 0:
                    link(v.tensor_scalar(sig[:, :], sig[:, :], 1.0, None, ALU.add))
                link(v.tensor_reduce(gm[:, :], gates[:, :, :], AX.X, ALU.add))
                yield
                dve.sync(v)
                link(v.reciprocal(gm[:, :], gm[:, :]))
                if n == 0:
                    link(v.reciprocal(sig[:, :], sig[:, :]))
                yield
                dve.sync(v)
                link(v.tensor_tensor(gates[:, :, :], gates[:, :, :], per_tile(gm[:, :]), ALU.mult))
                src = gates
                for j in range(picks):
                    yield
                    dve.sync(v)
                    link(v.tensor_reduce(wk[:, j, :], src[:, :, :], AX.X, ALU.max))
                    yield
                    dve.sync(v)
                    link(v.tensor_tensor(cand[:, :, :], src[:, :, :], per_tile(wk[:, j, :]), ALU.is_equal))
                    yield
                    dve.sync(v)
                    link(v.tensor_tensor(cand[:, :, :], cand[:, :, :], per_expert(cst("first")), ALU.mult))
                    yield
                    dve.sync(v)
                    link(v.tensor_reduce(gm[:, :], cand[:, :, :], AX.X, ALU.max))
                    yield
                    dve.sync(v)
                    link(v.tensor_tensor(pick[j][:, :, :], cand[:, :, :], per_tile(gm[:, :]), ALU.is_equal))
                    if j + 1 < picks:
                        yield
                        dve.sync(v)
                        link(v.scalar_tensor_tensor(out=g2[:, :, :], in0=pick[j][:, :, :], scalar=-2.0,
                                                    in1=gates[:, :, :], op0=ALU.mult, op1=ALU.add))
                        src = g2
                yield
                dve.sync(v)
                if picks == 2:
                    ins = v.tensor_tensor(both16[:, :, :], pick[0][:, :, :], pick[1][:, :, :], ALU.add)
                else:
                    ins = v.tensor_copy(both16[:, :, :], pick[0][:, :, :])
                ins.then_inc(s_picked, 1)
                yield "picked"
                wait(v, s_ranked, 1 + 2 * n)
                v.tensor_copy(tot16[:, :], B_TOT).then_inc(s_picked, 1)
                yield "totals"
                wait(v, s_ranked, 2 + 2 * n)
                link(v.tensor_copy(counts[:, :], B_CNT))
                v.tensor_copy(rank[:, :, :], B_RANK.rearrange("p (i e) -> p i e", e=E)).then_inc(s_rank, 1)
                yield "ranked"
                dve.sync(v)
                link(v.tensor_tensor(stepcmp[:, :, :], counts[:, :].unsqueeze(2).broadcast_to([P, E, NT]),
                                     cst("steps").unsqueeze(1).broadcast_to([P, E, NT]), ALU.is_gt))
                yield
                dve.sync(v)
                link(v.tensor_reduce(ntile[:, :], stepcmp[:, :, :], AX.X, ALU.add))
                link(v.memset(start_[:, :], 1.0))
                yield
                dve.sync(v)
                link(v.tensor_tensor_scan(cum[:, :], start_[:, :], ntile[:, :], 0.0, ALU.mult, ALU.add))
                yield
                dve.sync(v)
                link(v.tensor_tensor(start_[:, :], cum[:, :], ntile[:, :], ALU.subtract))
                link(v.tensor_tensor(tilecmp[:, 0:T, :],
                                     cst("tiles")[:, 0:T].unsqueeze(2).broadcast_to([P, T, E - 1]),
                                     cum[:, 0:E - 1].unsqueeze(1).broadcast_to([P, T, E - 1]), ALU.is_ge))
                yield
                dve.sync(v)
                link(v.tensor_scalar(start_[:, :], start_[:, :], float(P), None, ALU.mult))
                link(v.tensor_reduce(tef[:, 0:T], tilecmp[:, 0:T, :], AX.X, ALU.add))
                yield
                dve.sync(v)
                wait(v, s_rank, n + 1)
                link(v.tensor_tensor(g2[:, :, :], rank[:, :, :], per_expert(start_[:, :]), ALU.add))
                link(v.tensor_copy(te[:, 2:T + 2], tef[:, 0:T]))
                for j in range(picks):
                    yield
                    dve.sync(v)
                    link(v.tensor_tensor(cand[:, :, :], g2[:, :, :], pick[j][:, :, :], ALU.mult))
                    yield
                    dve.sync(v)
                    link(v.tensor_reduce(posf[:, :], cand[:, :, :], AX.X, ALU.add))
                    yield
                    dve.sync(v)
                    link(v.tensor_copy(pos[:, j, :], posf[:, :]))
                yield
                dve.sync(v)
                v.sem_inc(s_route, 1)

            @on("scalar")
            def _(s):
                wait(s, s_ex, 1 + 2 * n)
                if n == 0:
                    s.activation(sig[:, :], lg[:, :, E], ACT.Exp, scale=-1.0)
                s.activation(gates[:, :, :], gates[:, :, :], ACT.Exp).then_inc(s_ex, 1)

            def tensor_steps(t):
                wait(t, s_picked, 1 + 2 * n)
                flat = both16[:, :, :].rearrange("p i e -> p (i e)")
                t.matmul(B_TOT, flat, ones16[:, :], start=True, stop=True).then_inc(s_ranked, 1)
                yield
                wait(t, s_picked, 2 + 2 * n)
                t.matmul(B_RANK, before16[:, :], flat, start=True, stop=False)
                t.matmul(B_RANK, tot16[:, :], tile_before16[:, :], start=False, stop=True)
                t.matmul(B_CNT, tot16[:, :], same16[:, :], start=True, stop=True).then_inc(s_ranked, 1)
                yield
                wait(t, s_rank, n + 1)

            def scatter(g):
                wait(g, s_route, n + 1)
                wait_dma(g, s_slot_init, N_INIT)
                for j in range(picks):
                    if j:
                        wait_scatter(g, s_scat[n], NT * j)
                    pool.inc(g.tensor_copy(xr[:, :, P], wk[:, j, :]))
                    pool.inc(g.tensor_copy(xr[:, :, P + 1].bitcast(U32), cst("token")[:, j * NT:(j + 1) * NT].bitcast(U32)))
                    pool.sync(g)
                    for i in range(NT):
                        g.indirect_dma_start(out=slots[n], out_offset=bass.IndirectOffsetOnAxis(ap=pos[:, j, i:i + 1], axis=0),
                                             in_=xr[:, i, :], in_offset=None).then_inc(s_scat[n], 16)
            return vector_steps, tensor_steps, scatter

        s_scat = [sem(f"s_scat{n}", software_dma=True) for n in range(2)]
        s_lg = sem("s_lg")
        route0_dve, route0_pe, route0_scatter = routing(0, K0, T0)

        s_stk = [sem(f"s_stk{k}") for k in range(2)]
        s_m = [sem(f"s_m{k}") for k in range(2)]
        s_s1 = sem("s_s1")
        s_mx = sem("s_mx")
        s_mt = sem("s_mt")
        s_mp = sem("s_mp")
        s_s2 = sem("s_s2")
        s_p = sem("s_p")
        s_pv = sem("s_pv")
        s_oq = sem("s_oq")
        s_tok = sem("s_tok")
        s_on = sem("s_on")
        s_ot = sem("s_ot")
        s_oT = sem("s_oT")
        s_wo = sem("s_wo")
        s_x1 = sem("s_x1")
        s_pvz = sem("s_pvz")
        s_v0 = sem("s_v0")
        NG = H0 // HG
        NU = H0 // 2 * C
        mx = [sb(f"mx{k}", [P, H0, C]) for k in range(2)]
        mr = sb("mr", [C * H0, P])
        mp = sb("mp", [C * H0, 3, P], BF16)
        p32 = [[region("attention", [HG, S]) for c in range(C)] for g in range(2)]
        v_row = [region("attention", [C, H0, VC]) for k in range(2)]
        oq = [region("attention", [2, S]) for hf in range(2)]
        den = sb("den", [P, C, 2 * HG])
        onorm = sb("onorm", [P, C, P])
        oT = sb("oT", [P, C, P])
        B_S2 = [psum[:, 0:2, :], psum[:, 2:4, :]]
        B_S1 = [bank[4], bank[5]]
        B_PV, B_M = bank[6], bank[7]

        def take_v(g, b, k):
            wait(g, s_pv, (b - 1) * NG)
            g.tensor_copy(v_row[k][:, :, :, :], v0[:, at(b * C, C), :, :]).then_inc(s_v0, 1)

        @on("gpsimd")
        def _(g):
            wait(g, s_vp, B)
            wait_dma(g, s_slot_init, N_INIT)
            for b in range(2):
                take_v(g, b, b)
            route0_scatter(g)
            pairs(g, None, 0, lambda b, k, half: take_v(g, b, k), peel=1, first=False)

        @on("sync")
        def _(sp):
            wait(sp, s_stack0, 4)
            wait_dma(sp, s_fixed_out, 2)

            def load(b, k, half):
                wait_dma(sp, s_qst[k], (half + 1) * NP0)
                wait(sp, s_s2, (b - 1) * NG * C)
                for z, stack in enumerate((stQ[k], stK[k])):
                    sp.dma_start(stack[0:SROW, :, :].rearrange("p h s -> p (h s)"), qk_scr[b, z]).then_inc(s_stk[k], 16)

            def maxima(b, k):
                for t in range(3):
                    wait(sp, s_mp, b * 3 + t + 1)
                    sp.dma_start(stQ[k][MROW + t:MROW + t + 1, :, :].rearrange("o h (c s) -> o (h c) s", c=C),
                                 mp[:, t, :]).then_inc(s_m[k], 16)
            load(0, 0, 0)
            load(1, 1, 0)
            late_loads(sp)
            maxima(0, 0)

            def step(b, k, half):
                if is_last(b):
                    return
                maxima(b + 1, 1 - k)
                if not (isinstance(b, int) and b + 2 >= B):
                    load(b + 2, k, half + 1)
            pairs(sp, None, 0, step)
        N_STK, N_M = 2, 3

        UNITS = ((0, 5), (5, 11), (11, 16), (16, 16))

        def before(b, k):
            return None if isinstance(b, int) and b == 0 else (b - 1, 1 - k)

        @on("tensor")
        def _(t):
            wait(t, s_sh, B)

            def scores_max(b, k, half, u):
                if u == 0:
                    wait_dma(t, s_stk[k], (half + 1) * N_STK)
                wait(t, s_mx, b * NU + u - 1)
                hp, c = divmod(u, C)
                for n in range(2):
                    h = 2 * hp + n
                    mm = t.matmul(B_S1[u % 2][:, n * S:(n + 1) * S], stQ[k][:, h, c * P:(c + 1) * P], stK[k][:, h, :],
                                  start=True, stop=True)
                mm.then_inc(s_s1, 1)

            def turn_maxima(b, k):
                wait(t, s_mx, (b + 1) * NU)
                wait(t, s_x1, b - 1)
                t.transpose(B_M[0:C * H0, 0:P], mx[k][:, :, :].rearrange("p h c -> p (h c)"), ident).then_inc(s_mt, 1)

            def scores(b, k, half, g):
                if g == 0:
                    wait_dma(t, s_m[k], (half + 1) * N_M)
                for c in range(C):
                    wait(t, s_p, (b * NG + g) * C + c - 1)
                    for n in range(HG):
                        h = g * HG + n
                        mm = t.matmul(B_S2[c][:, n // 2, n % 2 * S:(n % 2 + 1) * S], stK[k][:, h, c * P:(c + 1) * P],
                                      stQ[k][:, h, :], start=True, stop=True)
                    mm.then_inc(s_s2, 1)

            def values(b, k, g):
                wait(t, s_p, (b * NG + g + 1) * C)
                wait(t, s_oq, b * NG + g)
                if g == 0:
                    wait(t, s_v0, b + 1)
                for c in range(C):
                    for n in range(HG):
                        mm = t.matmul(B_PV[32 * n:32 * n + VC, 0:S], v_row[k][:, c, g * HG + n, :], p32[g % 2][c][:, n, :],
                                      start=(c == 0), stop=(c == C - 1))
                mm.then_inc(s_pv, 1)

            def turn_values(b, hf):
                wait(t, s_oq, b * NG + 2 * hf + 2)
                if hf:
                    wait(t, s_on, 2 * b + 1)
                else:
                    wait(t, s_mp, (b + 2) * 3 if not is_last(b) else B * 3)
                    wait(t, s_x1, b)
                for j in range(2):
                    for c in range(C):
                        mm = t.transpose(B_M[:, c * S + j * P:c * S + (j + 1) * P], oq[hf][:, j, c * P:(c + 1) * P], ident)
                mm.then_inc(s_tok, 1)

            def turn_outputs(b):
                wait(t, s_on, 2 * b + 2)
                for c in range(C):
                    mm = t.transpose(B_M[:, c * P:(c + 1) * P], onorm[:, c, :], ident)
                mm.then_inc(s_ot, 1)

            def project(b):
                wait(t, s_oT, b + 1)
                for c in range(C):
                    mm = t.matmul(B_M[:, c * P:(c + 1) * P], oT[:, c, :], w_qkvo[:, 3, :], start=True, stop=True)
                mm.then_inc(s_wo, 1)

            wait(t, s_pvz, 1)
            route = route0_pe(t)
            for u in range(NU):
                scores_max(0, 0, 0, u)
                if u in (13, 15):
                    next(route, None)
            next(route, None)
            turn_maxima(0, 0)

            def step(b, k, half):
                nhalf = half + k
                prev = before(b, k)

                def units(g):
                    if not is_last(b):
                        for u in range(*UNITS[g]):
                            scores_max(b + 1, 1 - k, nhalf, u)
                scores(b, k, half, 0)
                if prev:
                    values(*prev, 3)
                units(0)
                if prev:
                    turn_values(prev[0], 1)
                scores(b, k, half, 1)
                if prev:
                    turn_outputs(prev[0])
                values(b, k, 0)
                units(1)
                if prev:
                    project(prev[0])
                scores(b, k, half, 2)
                values(b, k, 1)
                units(2)
                if not is_last(b):
                    turn_maxima(b + 1, 1 - k)
                scores(b, k, half, 3)
                values(b, k, 2)
                turn_values(b, 0)

            pairs(t, None, 0, step, peel=1)
            values(B - 1, 1, 3)
            turn_values(B - 1, 1)
            turn_outputs(B - 1)
            project(B - 1)

        @on("scalar")
        def _(s):
            def take_values(b, g):
                wait(s, s_pv, b * NG + g + 1)
                if g % 2 == 0:
                    wait(s, s_tok, 2 * b + g // 2 - 1)
                s.copy(oq[g // 2][:, g % 2, :], B_PV[:, 0:S]).then_inc(s_oq, 1)

            def step(b, k, half):
                prev = before(b, k)
                for g in range(NG):
                    for c in range(C):
                        n = (b * NG + g) * C + c
                        wait(s, s_s2, n + 1)
                        wait(s, s_pv, b * NG + g - 1)
                        s.activation(p32[g % 2][c][:, :, :].rearrange("p h s -> p (h s)"),
                                     B_S2[c].rearrange("p n s -> p (n s)"), ACT.Exp, scale=SCALE0).then_inc(s_p, 1)
                    if g:
                        take_values(b, g - 1)
                    elif prev:
                        take_values(prev[0], NG - 1)
            wait_dma(s, s_slot_init, N_INIT)
            pairs(s, None, 0, step, peel=1)
            take_values(B - 1, NG - 1)

        @on("vector")
        def _(v):
            def maximum(b, k, u):
                hp, c = divmod(u, C)
                wait(v, s_s1, b * NU + u + 1)
                if u == 0:
                    wait(v, s_mt, b - 1)
                v.tensor_reduce(mx[k][:, 2 * hp:2 * hp + 2, c], B_S1[u % 2].rearrange("p (n s) -> p n s", n=2), AX.X,
                                ALU.max).then_inc(s_mx, 1)

            def maxima_parts(b, k, half):
                wait(v, s_mt, b + 1)
                if not (isinstance(b, int) and b == 0):
                    wait_dma(v, s_m[1 - k], (half + k) * N_M)
                m = B_M[0:C * H0, 0:P]
                v.tensor_copy(mp[:, 0, :], m).then_inc(s_mp, 1)
                wait(v, s_mp, 3 * b + 1)
                dve.link(v, v.tensor_tensor(mr[:, :], m, mp[:, 0, :], ALU.subtract))
                v.tensor_copy(mp[:, 1, :], mr[:, :]).then_inc(s_mp, 1)
                wait(v, s_mp, 3 * b + 2)
                v.tensor_tensor(mp[:, 2, :], mr[:, :], mp[:, 1, :], ALU.subtract).then_inc(s_mp, 1)

            def divide(b, hf):
                wait(v, s_tok, 2 * b + hf + 1)
                tok = B_M.rearrange("p (c n q) -> p c n q", c=C, q=32)
                dve.link(v, v.reciprocal(den[:, :, :], tok[:, :, :, D0]))
                if hf == 0:
                    wait(v, s_ot, b)
                half_cols = onorm[:, :, hf * 2 * HG * D0:(hf + 1) * 2 * HG * D0].rearrange("p c (n d) -> p c n d", d=D0)
                v.tensor_tensor(half_cols, tok[:, :, :, 0:D0],
                                den[:, :, :].unsqueeze(3).broadcast_to([P, C, 2 * HG, D0]), ALU.mult).then_inc(s_on, 1)

            def outputs(b):
                wait(v, s_ot, b + 1)
                wait(v, s_wo, b)
                v.tensor_copy(oT[:, :, :].rearrange("p c n -> p (c n)"), B_M[:, 0:C * P]).then_inc(s_oT, 1)

            def add_to_stream(b):
                wait(v, s_wo, b + 1)
                tiles = at(b * C, C)
                v.tensor_tensor(x_sb[:, tiles, :], B_M[:, 0:C * P].rearrange("p (c n) -> p c n", c=C), x_sb[:, tiles, :],
                                ALU.add).then_inc(s_x1, 1)

            route = route0_dve(v)
            v.memset(B_PV, 0.0).then_inc(s_pvz, 1)
            turns = 0
            for u in range(NU):
                maximum(0, 0, u)
                if u < 12 and turns < 100:
                    next(route)
                    turns += 1
                    if next(route) == "picked":
                        turns = 100
                if u == 12:
                    while turns < 100 and next(route) != "picked":
                        pass
                if u in (14, 15):
                    next(route)
            for _ in route:
                pass
            maxima_parts(0, 0, 0)

            def step(b, k, half):
                prev = before(b, k)

                def units(g):
                    if not is_last(b):
                        for u in range(*UNITS[g]):
                            maximum(b + 1, 1 - k, u)
                units(0)
                if prev:
                    divide(prev[0], 1)
                    outputs(prev[0])
                units(1)
                if prev:
                    add_to_stream(prev[0])
                units(2)
                if not is_last(b):
                    maxima_parts(b + 1, 1 - k, half + k)
                divide(b, 0)

            pairs(v, dve, 2 * 3, step, peel=1)
            divide(B - 1, 1)
            outputs(B - 1)
            add_to_stream(B - 1)

        xs = [sb(f"xs{r}", [P, ROW]) for r in range(4)]
        ends = [sb(f"ends{r}", [P, 2]) for r in range(4)]
        xsT = [sb(f"xsT{k}", [P, P]) for k in range(2)]
        act_t = [sb(f"act_t{k}", [P, HID1]) for k in range(2)]
        hid = [sb(f"hid{k}", [P, HID1]) for k in range(2)]
        hidT = [sb(f"hidT{k}", [P, HID1]) for k in range(2)]
        y = [sb(f"y{r}", [P, P]) for r in range(4)]
        y0 = [sb(f"yb{r}", [P, P]) for r in range(2)]
        names = ("tx", "en", "xT", "up", "ac", "hd", "ht", "hT", "dn", "y")

        def experts(n, T):
            q = {m: sem(f"e{n}_{m}") for m in names}
            q_part = sem(f"e{n}_part")
            q_ld = [sem(f"e{n}_ld{r}") for r in range(4)]
            q_sc = [sem(f"e{n}_sc{r}", software_dma=True) for r in range(4)]
            KC = 2 if n == 0 else 4
            B_X, B_G2, B_H, B_Y = bank[0:2], bank[2:4], bank[4:6], bank[6:8]

            e = []

            def steps(eng, chain, k, step, with_experts=False):
                def load(t):
                    if with_experts:
                        e[:] = nc.values_load_multi_w_load_instructions(te[0:1, at(t, 6)], engines=[eng.engine],
                                                                        min_val=0, max_val=E - 1)[1]
                load(0)
                for t in range(0, 4):
                    step(t, t, 0)

                def body(i):
                    load(i * 4 + 4)
                    for r in range(4):
                        step(i * 4 + 4 + r, r, i + 1)
                if chain is None:
                    with eng.Fori(0, T // 4 - 2) as i:
                        body(i)
                else:
                    chain.loop(eng, T // 4 - 2, k, body)
                for t in range(T - 4, T + 2):
                    if t % 4 == 0:
                        load(t)
                    step(t, t % 4, t // 4)

            def ring(r, turn, d):
                return (r + d) % 4, turn + (r + d) // 4

            def has(t):
                return not isinstance(t, int) or 0 <= t < T

            @on("sync")
            def _(sp):
                wait_scatter(sp, s_scat[n], NT * (K0 if n == 0 else 1))

                def load(t, r):
                    if has(t):
                        wait(sp, q["tx"], t - 3)
                        wait(sp, q["en"], t - 3)
                        sp.dma_start(xs[r][:, :], slots[n][at(t * P, P), :]).then_inc(q_ld[r], 16)
                for t in range(4):
                    load(t, t)

                def step(t, r, turn):
                    load(t + 4, r)
                    if n == 0 and r == 0 and not isinstance(t, int):
                        e = turn - 1
                        sp.dma_start(w_up1[:, at(e, 1), :], a["w1"].rearrange("e p n -> p e n")[:, at(e, 1), :]).then_inc(s_exp1, 16)
                        sp.dma_start(w_dn1[:, :, at(e, 1), :].rearrange("p c o n -> p (c o) n"),
                                     a["w2"][at(e, 1), :, :].rearrange("o (c p) n -> p (o c) n", p=P)).then_inc(s_exp1, 16)
                        sp.dma_start(b_up1[:, at(e, 1), :], a["b1"][at(e, 1), :].broadcast_to([P, HID1]).unsqueeze(1)).then_inc(s_exp1, 16)
                        sp.dma_start(b_dn1[:, at(e, 1), :], a["b2"][at(e, 1), :].broadcast_to([P, P]).unsqueeze(1)).then_inc(s_exp1, 16)
                if n == 0:
                    wait(sp, s_x1, B)
                steps(sp, None, 0, step)

            @on("tensor")
            def _(pe):
                wait_dma(pe, s_exp0 if n == 0 else s_exp1, N_EXP0 if n == 0 else N_EXP1)
                wait(pe, s_x1 if n == 0 else s_x2, B)

                def turn_x(t, r, turn):
                    if has(t):
                        wait_dma(pe, q_ld[r], turn + 1)
                        wait(pe, q["xT"], t - 1)
                        pe.transpose(B_X[r % 2][:, 0:P], xs[r][:, 0:P], ident).then_inc(q["tx"], 1)

                def step(t, r, turn):
                    turn_x(t + 1, *ring(r, turn, 1))
                    if has(t):
                        k = r % 2
                        wait(pe, q["xT"], t + 1)
                        wait(pe, q["hd"] if n == 0 else q["ac"], t - 1)
                        if n == 0:
                            pe.matmul(B_G2[k][:, 0:2 * I0], xsT[k][:, :], w_gu0[:, e[r + 2], :], start=True, stop=True).then_inc(q["up"], 1)
                        else:
                            pe.matmul(B_G2[k][:, :], xsT[k][:, :], w_up1[:, e[r + 2], :], start=True, stop=True).then_inc(q["up"], 1)
                    if has(t - 1):
                        k = (r - 1) % 2
                        wait(pe, q["hd"], t)
                        wait(pe, q["hT"], t - 2)
                        for j in range(KC):
                            mm = pe.transpose(B_H[k][:, j * P:(j + 1) * P], hid[k][:, j * P:(j + 1) * P], ident)
                        mm.then_inc(q["ht"], 1)
                    if has(t - 2):
                        k = r % 2
                        wait(pe, q["hT"], t - 1)
                        wait(pe, q["y"], t - 3)
                        for j in range(KC):
                            w = w_dn0[:, e[r], j, :] if n == 0 else w_dn1[:, j, e[r], :]
                            mm = pe.matmul(B_Y[k][:, 0:P], hidT[k][:, j * P:(j + 1) * P], w, start=(j == 0), stop=(j == KC - 1))
                        mm.then_inc(q["dn"], 1)
                turn_x(0, 0, 0)
                steps(pe, None, 0, step, with_experts=True)

            @on("scalar")
            def _(s):
                def take_x(t, r):
                    if has(t):
                        wait(s, q["tx"], t + 1)
                        wait(s, q["up"], t - 1)
                        s.copy(xsT[r % 2][:, :], B_X[r % 2][:, 0:P]).then_inc(q["xT"], 1)

                def step(t, r, turn):
                    take_x(t + 1, (r + 1) % 4)
                    if has(t):
                        k = r % 2
                        if n == 0:
                            wait(s, q["up"], t + 1)
                            wait(s, q["hd"], t - 1)
                            s.activation(act_t[k][:, 0:I0], B_G2[k][:, 0:I0], ACT.Silu).then_inc(q["ac"], 1)
                        else:
                            wait(s, q["ac"], t + 1)
                            wait(s, q["ht"], t - 1)
                            s.activation(hid[k][:, :], act_t[k][:, :], ACT.Gelu).then_inc(q["hd"], 1)
                    if has(t - 1):
                        k = (r - 1) % 2
                        wait(s, q["ht"], t)
                        wait(s, q["dn"], t - 2)
                        s.copy(hidT[k][:, 0:KC * P], B_H[k][:, 0:KC * P]).then_inc(q["hT"], 1)
                take_x(0, 0)
                steps(s, None, 0, step)

            @on("vector")
            def _(v):
                wait(v, s_route, n + 1)
                if n == 0:
                    wait(v, s_x1, B)
                    for k in range(2):
                        dve.link(v, v.memset(hid[k][:, I0:2 * P], 0.0))

                def step(t, r, turn):
                    if n == 0 and not isinstance(t, int):
                        merge_shared(v, turn - 1, r)
                    if has(t):
                        wait_dma(v, q_ld[r], turn + 1)
                        wait_scatter(v, q_sc[r], turn)
                        v.tensor_copy(ends[r][:, :].bitcast(U32), xs[r][:, P:P + 2].bitcast(U32)).then_inc(q["en"], 1)
                        k = r % 2
                        wait(v, q["up"], t + 1)
                        if n == 0:
                            wait(v, q["ac"], t + 1)
                            wait(v, q["ht"], t - 1)
                            v.tensor_tensor(hid[k][:, 0:I0], act_t[k][:, 0:I0], B_G2[k][:, I0:2 * I0], ALU.mult).then_inc(q["hd"], 1)
                        else:
                            wait(v, q["hd"], t - 1)
                            v.tensor_tensor(act_t[k][:, :], B_G2[k][:, :], b_up1[:, e[r + 2], :], ALU.add).then_inc(q["ac"], 1)
                    if has(t - 2):
                        rr, _ = ring(r, turn, -2)
                        wait(v, q["dn"], t - 1)
                        wait(v, q["en"], t - 1)
                        src = B_Y[r % 2][:, 0:P]
                        if n:
                            dve.link(v, v.tensor_tensor(y0[r % 2][:, :], src, b_dn1[:, e[r], :], ALU.add))
                            src = y0[r % 2][:, :]
                        v.tensor_scalar(y[rr][:, :], src, ends[rr][:, 0:1], None, ALU.mult).then_inc(q["y"], 1)
                steps(v, dve, 4 if n else 2, step, with_experts=(n == 1))

            @on("gpsimd")
            def _(g):
                def step(t, r, turn):
                    if has(t - 2):
                        rr, _ = ring(r, turn, -2)
                        wait(g, q["en"], t - 1)
                        wait(g, q["y"], t - 1)
                        g.sem_inc(q_part, 1)
                        g.indirect_dma_start(out=ys[n], out_offset=bass.IndirectOffsetOnAxis(
                            ap=ends[rr][:, 1:2].bitcast(U32), axis=0), in_=y[rr][:, :], in_offset=None).then_inc(q_sc[rr], 16)
                steps(g, None, 0, step)
            return q_sc

        s_x2 = sem("s_x2")

        s_merged = sem("s_merged")

        def merge_shared(v, turn, r):
            rows = at(turn * 2, 2)
            wide = [P, 2, P]
            if r:
                dve.sync(v)
            if r == 0:
                dve.inc(v.tensor_tensor(side[:, rows, :], side[:, rows, :], sig[:, rows].unsqueeze(2).broadcast_to(wide), ALU.mult))
            elif r == 1:
                dve.inc(v.tensor_tensor(side[:, rows, :], side[:, rows, :], bo_row[:, :].unsqueeze(1).broadcast_to(wide), ALU.add))
            elif r == 2:
                v.tensor_tensor(x_sb[:, rows, :], x_sb[:, rows, :], side[:, rows, :], ALU.add).then_inc(s_merged, 1)
        assert T0 // 4 - 2 == NT // 2

        s_sc0 = experts(0, T0)

        s_xn1 = sem("s_xn1")
        s_xr1 = sem("s_xr1")
        s_tx1 = sem("s_tx1")
        s_xT1 = sem("s_xT1")
        s_red = sem("s_red")
        s_redT = sem("s_redT")
        s_lgm = sem("s_lgm")
        redT = [bench.take("attention", [S], partitions=GD) for k in range(2)]
        B_RED, B_LG = bank[1], bank[2]

        s_side = [sem(f"s_side{n}") for n in range(4)]
        out_k = (side[:, :, :], xnT1[:, :].rearrange("p (i d) -> p i d", d=P))
        N4 = NT // 4

        @on("sync")
        def _(sp):
            for q in s_sc0:
                wait_scatter(sp, q, T0 // 4)
            wait(sp, s_merged, T0 // 4 - 2)
            for n in range(4):
                rows = slice(n * N4, (n + 1) * N4)
                for j in range(K0):
                    sp.dma_start(out_k[j][:, rows, :], ys[0][j * NTOK:(j + 1) * NTOK, :].rearrange("(i p) d -> p i d", p=P)[:, rows, :]).then_inc(s_side[n], 16)

        def add_expert_outputs(v, n):
            rows = slice(n * N4, (n + 1) * N4)
            wait_dma(v, s_side[n], K0)
            for j in range(K0):
                dve.link(v, v.tensor_tensor(x_sb[:, rows, :], x_sb[:, rows, :], out_k[j][:, rows, :], ALU.add))
        layer_stats(1, add_expert_outputs)

        @on("vector")
        def _(v):
            normalise(v, 0, 0, s_xn1)

            def step(b, k, half):
                if not is_last(b):
                    wait(v, s_tx1, b)
                    wait(v, s_xr1, b)
                    normalise(v, b + 1, 1 - k, s_xn1)
                wait(v, s_lgm, b + 1)
                v.tensor_copy(lg[:, at(b * C, C), 0:E], B_LG[:, 0:C * E].rearrange("p (c e) -> p c e", c=C)).then_inc(s_lg, 1)
            pairs(v, None, 0, step)

        @on("gpsimd")
        def _(g):
            wait_scatter(g, s_scat[0], NT * K0)
            def step(b, k, half):
                wait(g, s_xn1, b + 1)
                g.tensor_copy(xr[:, at(b * C, C), 0:P], xn[k][:, :, :]).then_inc(s_xr1, 1)
            pairs(g, None, 0, step)

        @on("scalar")
        def _(s):
            def take_xT(b, k):
                wait(s, s_tx1, b + 1)
                s.copy(xnT1[:, at(b * S, S)], B_T[:, 0:S]).then_inc(s_xT1, 1)
            take_xT(0, 0)

            def step(b, k, half):
                wait(s, s_red, b + 1)
                wait(s, s_lgm, b - 1)
                s.copy(redT[k][:, :], B_RED[0:GD, 0:S]).then_inc(s_redT, 1)
                if not is_last(b):
                    take_xT(b + 1, 1 - k)
            pairs(s, None, 0, step)

        @on("tensor")
        def _(t):
            for q in s_sc0:
                wait_scatter(t, q, T0 // 4)

            def turn(b, k):
                wait(t, s_xn1, b + 1)
                wait(t, s_xT1, b)
                for c in range(C):
                    mm = t.transpose(B_T[:, c * P:(c + 1) * P], xn[k][:, c, :], ident)
                mm.then_inc(s_tx1, 1)
            turn(0, 0)
            wait(t, s_wg, 4)
            wait_dma(t, s_w1, N_W1)

            def step(b, k, half):
                wait(t, s_xT1, b + 1)
                wait(t, s_redT, b)
                t.matmul(B_RED[0:GD, 0:S], w_red1[:, :], xnT1[:, at(b * S, S)], start=True, stop=True).then_inc(s_red, 1)
                if not is_last(b):
                    turn(b + 1, 1 - k)
                wait(t, s_redT, b + 1)
                wait(t, s_lg, b)
                for c in range(C):
                    mm = t.matmul(B_LG[:, c * E:(c + 1) * E], redT[k][:, c * P:(c + 1) * P], wgT[:, :], start=True, stop=True)
                mm.then_inc(s_lgm, 1)
            pairs(t, None, 0, step)

        route1_dve, route1_pe, route1_scatter = routing(1, 1, T1)

        s_xb = sem("s_xb")
        s_kv = sem("s_kv")
        s_kT = sem("s_kT")
        s_Q = sem("s_Q")
        s_q = sem("s_q")
        s_S = sem("s_S")
        s_nm = sem("s_nm")
        s_P = sem("s_P")
        s_Pn = sem("s_Pn")
        s_T = sem("s_T")
        s_PT = sem("s_PT")
        s_V = sem("s_V")
        s_o = sem("s_o")
        s_W = sem("s_W")
        LEFT = P + S
        xb = [bench.take("attention", [S]) for k in range(2)]
        kT = [bench.take("attention", [S]) for k in range(2)]
        v1 = [bench.take("attention", [S]) for k in range(2)]
        qT = [bench.take("attention", [S]) for k in range(2)]
        prob = [bench.take("attention", [LEFT]) for r in range(4)]
        probT = [bench.take("attention", [LEFT]) for k in range(2)]
        rowmax = [sb(f"rowmax{k}", [P, C]) for k in range(2)]
        negmax = [sb(f"negmax{r}", [P, C]) for r in range(4)]
        rowsum = [sb(f"rowsum{r}", [P, C]) for r in range(4)]
        oT1 = [bench.take("attention", [H1, S]) for k in range(2)]
        pe_T = cst("pe")
        B_Q, B_O, B_S, B_TT, B_W = bank[0], (bank[1], bank[6]), bank[2:4], bank[4:6], bank[7]
        TURNS = (slice(0, P), slice(P, 2 * P), slice(2 * P, 3 * P))

        def heads(eng, chain, k_links, stages, extra=()):
            def run(b, k, h, upto):
                for lag, f in stages:
                    hh = h - lag
                    bb, kk = (b, k) if 0 <= hh < H1 else (b - 1, 1 - k)
                    if hh >= H1 or (isinstance(bb, int) and bb < 0):
                        continue
                    hh %= H1
                    f(bb, kk, hh, bb * H1 + hh)

            def step(b, k, half):
                for h in range(H1):
                    run(b, k, h, H1)
                    for where, f in extra:
                        if where == h:
                            f(b, k)
            pairs(eng, chain, k_links, step, peel=1)
            for h in range(4):
                for lag, f in stages:
                    hh = H1 + h - lag
                    if hh < H1:
                        f(B - 1, 1, hh, (B - 1) * H1 + hh)

        @on("gpsimd")
        def _(g):
            wait(g, s_xT1, 2)
            for b in range(2):
                g.tensor_copy(xb[b][:, :], xnT1[:, b * S:(b + 1) * S]).then_inc(s_xb, 1)

            def step(b, k, half):
                if not (isinstance(b, int) and b + 2 >= B):
                    wait(g, s_xT1, b + 3)
                    wait(g, s_kv, b + 1)
                    g.tensor_copy(xb[k][:, :], xnT1[:, at((b + 2) * S, S)]).then_inc(s_xb, 1)
            step(0, 0, 0)
            route1_scatter(g)
            step(1, 1, 0)
            pairs(g, None, 0, step, peel=1, first=False)

        @on("tensor")
        def _(t):
            wait(t, s_lg, B)

            def queries(b, k, h, H):
                wait(t, s_q, H)
                t.matmul(B_Q[:, 0:S], w_q1[:, h * P:(h + 1) * P], xnT1[:, at(b * S, S)], start=True, stop=True).then_inc(s_Q, 1)

            def keys_values(b, k):
                wait(t, s_xb, b + 1)
                t.matmul(B_W[:, 0:S], w_kv1[:, 0:P], xb[k][:, :], start=True, stop=True)
                for c in range(C):
                    mm = t.matmul(B_W[:, S + c * P:S + (c + 1) * P], xb[k][:, c * P:(c + 1) * P], w_kv1[:, P:2 * P], start=True, stop=True)
                mm.then_inc(s_kv, 1)

            def next_keys_values(b, k):
                if not is_last(b):
                    wait(t, s_x2, b)
                    keys_values(b + 1, 1 - k)

            def scores(b, k, h, H):
                wait(t, s_q, H + 1)
                wait(t, s_kT, b + 1)
                wait(t, s_P, H - 1)
                o, q = B_S[h % 2], qT[h % 2]
                t.matmul(o[:, 0:P], q[:, 0:P], kT[k][:, 0:P], start=True, stop=False)
                t.matmul(o[:, 0:P], ident16[:, :], mask16[:, :], start=False, stop=True)
                t.matmul(o[:, P:LEFT], q[:, P:S], kT[k][:, :], start=True, stop=False)
                t.matmul(o[:, 2 * P:LEFT], ident16[:, :], mask16[:, :], start=False, stop=True).then_inc(s_S, 1)

            def turn(b, k, h, H):
                wait(t, s_Pn, H + 1)
                wait(t, s_PT, H - 1)
                for cols in TURNS:
                    mm = t.transpose(B_TT[h % 2][:, cols], prob[h % 4][:, cols], ident)
                mm.then_inc(s_T, 1)

            def values(b, k, h, H):
                wait(t, s_PT, H + 1)
                wait(t, s_o, H - 1)
                pT, o = probT[h % 2], B_O[h % 2]
                t.matmul(o[:, 0:S], v1[k][:, 0:P], pT[:, 0:S], start=True, stop=False)
                t.matmul(o[:, P:S], v1[k][:, P:S], pT[:, S:LEFT], start=False, stop=True).then_inc(s_V, 1)

            def project(b, k):
                wait(t, s_o, (b + 1) * H1)
                wait(t, s_kT, b + 2 if not is_last(b) else B)
                for c in range(C):
                    for h in range(H1):
                        mm = t.matmul(B_W[:, c * P:(c + 1) * P], oT1[k][:, h, c * P:(c + 1) * P], w_o1[:, h, :],
                                      start=(h == 0), stop=(h == H1 - 1))
                mm.then_inc(s_W, 1)

            def last_project(b, k):
                if not isinstance(b, int) or b > 0:
                    project(b - 1, 1 - k)

            route = route1_pe(t)

            def route_step(b, k):
                if isinstance(b, int) and b == 0:
                    next(route, None)

            keys_values(0, 0)
            heads(t, None, 0, ((0, queries), (3, turn), (1, scores), (4, values)),
                  ((4, route_step), (5, route_step), (5, last_project), (7, route_step), (7, next_keys_values)))
            project(B - 1, 1)

        @on("vector")
        def _(v):
            def queries(b, k, h, H):
                wait(v, s_Q, H + 1)
                wait(v, s_S, H - 1)
                v.scalar_tensor_tensor(out=qT[h % 2][:, :], in0=B_Q[:, 0:S], scalar=b_q1[:, h:h + 1], in1=pe_T,
                                       op0=ALU.add, op1=ALU.add).then_inc(s_q, 1)

            def maxima(b, k, h, H):
                wait(v, s_S, H + 1)
                o = B_S[h % 2]
                dve.inc(v.tensor_reduce(rowmax[h % 2][:, 0:1], o[:, 0:P], AX.X, ALU.max))
                dve.link(v, v.tensor_reduce(rowmax[h % 2][:, 1:2], o[:, P:LEFT], AX.X, ALU.max))
                wait(v, s_P, H - 3)
                v.tensor_scalar(negmax[h % 4][:, :], rowmax[h % 2][:, :], -SCALE1, None, ALU.mult).then_inc(s_nm, 1)

            def divide(b, k, h, H):
                wait(v, s_P, H + 1)
                r = h % 4
                dve.link(v, v.reciprocal(rowsum[r][:, :], rowsum[r][:, :]))
                v.tensor_scalar(prob[r][:, 0:P], prob[r][:, 0:P], rowsum[r][:, 0:1], None, ALU.mult)
                v.tensor_scalar(prob[r][:, P:LEFT], prob[r][:, P:LEFT], rowsum[r][:, 1:2], None, ALU.mult).then_inc(s_Pn, 1)

            def take_T(b, k, h, H):
                wait(v, s_T, H + 1)
                wait(v, s_V, H - 1)
                v.tensor_copy(probT[h % 2][:, :], B_TT[h % 2][:, 0:LEFT]).then_inc(s_PT, 1)

            def keys_values(b, k):
                wait(v, s_kv, b + 1)
                v.scalar_tensor_tensor(out=kT[k][:, :], in0=B_W[:, 0:S], scalar=b_kv1[:, 0:1], in1=pe_T,
                                       op0=ALU.add, op1=ALU.add)
                v.tensor_copy(v1[k][:, :], B_W[:, S:2 * S]).then_inc(s_kT, 1)

            def next_keys_values(b, k):
                if not is_last(b):
                    keys_values(b + 1, 1 - k)

            def add_to_stream(b, k):
                wait(v, s_W, b + 1)
                rows = x_sb[:, at(b * C, C), :]
                v.tensor_tensor(rows, B_W[:, 0:S].rearrange("p (c n) -> p c n", c=C), rows, ALU.add).then_inc(s_x2, 1)

            def last_stream(b, k):
                if not isinstance(b, int) or b > 0:
                    add_to_stream(b - 1, 1 - k)

            route = route1_dve(v)
            pace = iter((3, 3, 3, 4, 1, 0, 1, 2) + (2,) * 8)

            def route_steps(b, k):
                if isinstance(b, int) and b <= 1:
                    for _ in range(next(pace)):
                        next(route, None)

            keys_values(0, 0)
            heads(v, dve, 2 * H1 * 3, ((0, queries), (3, take_T), (1, maxima), (2, divide)),
                  ((6, last_stream), (7, next_keys_values)) + tuple((h, route_steps) for h in range(H1)))
            assert next(route, None) is None
            add_to_stream(B - 1, 1)

        @on("scalar")
        def _(s):
            def exponentials(b, k, h, H):
                wait(s, s_nm, H + 1)
                wait(s, s_T, H - 3)
                r = h % 4
                for c, cols in enumerate((slice(0, P), slice(P, LEFT))):
                    ins = s.activation(prob[r][:, cols], B_S[h % 2][:, cols], ACT.Exp, bias=negmax[r][:, c:c + 1],
                                       scale=SCALE1, accum_out=rowsum[r][:, c:c + 1])
                ins.then_inc(s_P, 1)

            def outputs(b, k, h, H):
                wait(s, s_V, H + 1)
                wait(s, s_W, b - 1)
                s.activation(oT1[k][:, h, :], B_O[h % 2][:, 0:S], ACT.Identity, bias=b_kv1[:, 1:2]).then_inc(s_o, 1)
            heads(s, None, 0, ((1, exponentials), (4, outputs)))

        s_sc1 = experts(1, T1)

        s_piece = [sem(f"s_piece{n}") for n in range(4)]
        s_sum = sem("s_sum")
        s_out = [sem(f"s_out{n}") for n in range(4)]

        @on("sync")
        def _(sp):
            for q in s_sc1:
                wait_scatter(sp, q, T1 // 4)
            for n in range(4):
                sp.dma_start(side[:, n * N4:(n + 1) * N4, :],
                             ys[1][n * N4 * P:(n + 1) * N4 * P, :].rearrange("(i p) d -> p i d", p=P)).then_inc(s_piece[n], 16)
            for n in range(4):
                wait(sp, s_sum, n + 1)
                sp.dma_start(out.rearrange("(i p) d -> p i d", p=P)[:, n * N4:(n + 1) * N4, :],
                             x_sb[:, n * N4:(n + 1) * N4, :]).then_inc(s_out[n], 16)
            for n in range(4):
                wait_dma(sp, s_out[n], 1)

        @on("vector")
        def _(v):
            for n in range(4):
                wait_dma(v, s_piece[n], 1)
                rows = slice(n * N4, (n + 1) * N4)
                v.tensor_tensor(x_sb[:, rows, :], x_sb[:, rows, :], side[:, rows, :], ALU.add).then_inc(s_sum, 1)

        block = ctx.enter_context(nc.Block())

        @block.gpsimd
        def _(g):
            for s in sems:
                g.sem_inc(s, CREDIT)
            for f in parts["gpsimd"]:
                f(g)

        @block.sync
        def _(e):
            for f in parts["sync"]:
                f(e)

        @block.scalar
        def _(e):
            for f in parts["scalar"]:
                f(e)

        @block.vector
        def _(e):
            for f in parts["vector"]:
                f(e)

        @block.tensor
        def _(e):
            for f in parts["tensor"]:
                f(e)


def constants():
    import numpy as np
    cols, n = const_layout()
    c = np.zeros((P, n), np.float32)

    def put(name, value):
        c[:, cols[name][0]:cols[name][1]] = value

    r = np.arange(P)
    put("ident", np.eye(P))
    put("before", r[:, None] < r[None, :])
    put("tile_before", (r[:, None] % E == r[None, :] % E) & (r[:, None] // E < r[None, :] // E))
    put("same_expert", r[:, None] % E == np.arange(E)[None, :])
    put("first", E - np.arange(E)[None, :])
    put("steps", P * np.arange(NT)[None, :])
    put("tiles", np.arange(T0)[None, :])
    token = (np.arange(K0 * NT)[None, :] * P + r[:, None]).astype(np.uint32)
    put("token", token.view(np.float32))
    put("dump", (DUMP + np.arange(T0)[None, :] * P + r[:, None]).astype(np.uint32).view(np.float32))
    put("mask", np.where(r[None, :] > r[:, None], NEG, 0.0))
    pos = np.arange(S, dtype=np.float32)
    inv = np.exp(-np.log(10000.0) * np.arange(0, P, 2, dtype=np.float32) / P).astype(np.float32)
    ang = inv[:, None] * pos[None, :]
    pe = np.zeros((P, S), np.float32)
    pe[0::2], pe[1::2] = np.sin(ang), np.cos(ang)
    put("pe", pe)
    return c


def kernel(**inputs):
    import numpy as np
    import concourse.bacc as bacc
    from concourse.bass_utils import run_bass_kernel_spmd

    i = {k: np.asarray(v) for k, v in inputs.items()}

    def flat(x):
        return np.ascontiguousarray(x)

    def by_place(w):
        return w.reshape(-1, H0, D0).swapaxes(-1, -2).reshape(w.shape)

    arrays = {
        "x": flat(i["L0_attn_x"].reshape(NTOK, P)),
        "const": constants(),
        "Wq0": flat(by_place(i["L0_attn_Wq"])), "Wk0": flat(by_place(i["L0_attn_Wk"])), "Wv0": i["L0_attn_Wv"], "Wo0": i["L0_attn_Wo"],

        "bq0": flat(by_place(i["L0_attn_bq"])), "bk0": flat(by_place(i["L0_attn_bk"])), "bv0": i["L0_attn_bv"], "bo0": i["L0_attn_bo"],
        "gate0": flat(np.concatenate([i["L0_ffn_gate_w"], i["L0_ffn_shared_expert_gate_w"]]).T),
        "sgate": flat(i["L0_ffn_shared_gate_w"].T), "sup": flat(i["L0_ffn_shared_up_w"].T),
        "sdown": flat(i["L0_ffn_shared_down_w"].T),
        "gu0": flat(i["L0_ffn_experts_gate_up"].transpose(2, 0, 1)),
        "down0": flat(i["L0_ffn_experts_down"].transpose(0, 2, 1)),
        "Wq1": i["L1_attn_Wq"], "bq1": i["L1_attn_bq"], "Wkv1": i["L1_attn_Wkv"], "bkv1": i["L1_attn_bkv"],
        "Wo1": i["L1_attn_Wo"], "red1": flat(i["L1_ffn_wg_red"].T), "wg1": i["L1_ffn_wg"],
        "w1": i["L1_ffn_w1"], "w2": i["L1_ffn_w2"], "b1": i["L1_ffn_b1"],
        "b2": i["L1_ffn_b2"],
    }
    nc = bacc.Bacc("TRN2", target_bir_lowering=False, num_devices=1)
    aps = {k: nc.dram_tensor(k, v.shape, mybir.dt.from_np(v.dtype), kind="ExternalInput").ap() for k, v in arrays.items()}
    out = nc.dram_tensor("out", (NTOK, P), F32, kind="ExternalOutput").ap()
    build(nc, aps, out)
    r = run_bass_kernel_spmd(nc, [arrays], core_ids=[0])
    return r.results[0]["out"].reshape(B, S, P)
```

```python
from contextlib import ExitStack

import concourse.bass as bass
from concourse import mybir

ALU = mybir.AluOpType
ACT = mybir.ActivationFunctionType
AX = mybir.AxisListType
F32 = mybir.dt.float32
BF16 = mybir.dt.bfloat16
U32 = mybir.dt.uint32
I32 = mybir.dt.int32

P = 128
B, S = 8, 256
C = S // P
NT = B * C
NTOK = NT * P
EPS_LN = 1e-5
E = 8
CREDIT = 18

H0, D0 = 16, 8
I0 = 176
SI = 352
SJ = 3
K0 = 2
T0 = 40
QPARTS = (0, 0, 1, 0, 1, 2)
KPARTS = (0, 1, 0, 2, 1, 0)
PAIRS = tuple(tuple(zip([g for g, p in enumerate(QPARTS) if p == part], [g for g, p in enumerate(KPARTS) if p == part]))
              for part in range(3))
NP0 = len(QPARTS)
MROW = NP0 * D0
SROW = MROW + 3
VC = D0 + 1
SCALE0 = float(D0) ** -0.5

H1 = 8
HID1 = 512
T1 = 24
SCALE1 = float(P) ** -0.5
GD = 16
EPS_NORM = 1e-4
NEG = -3.0e38

EXPERT_TURN = (8, 4)
DUMP = K0 * NTOK
ROW = P + 2


def const_layout():
    at, out = 0, {}
    for name, n in (("ident", P), ("before", P), ("tile_before", P), ("same_expert", E), ("first", E),
                    ("steps", NT), ("tiles", T0), ("token", K0 * NT), ("dump", T0), ("mask", P), ("pe", S)):
        out[name] = (at, at + n)
        at += n
    return out, at


def build(nc, a, out):
    ctx = ExitStack()
    with ctx:
        sems = []

        def sem(name, software_dma=False):
            s = ctx.enter_context(nc.semaphore(name))
            if not software_dma:
                sems.append(s)
            return s

        def sb(name, shape, dt=F32):
            return ctx.enter_context(nc.sbuf_tensor("sb_" + name, shape, dt))

        def wait(eng, s, count):
            if not isinstance(count, int) or count > 0:
                eng.wait_ge(s, count + CREDIT)

        def wait_dma(eng, s, count):
            if not isinstance(count, int) or count > 0:
                eng.wait_ge(s, count * 16 + CREDIT)

        psum = ctx.enter_context(nc.psum_tensor("psum", [P, 8, 512], F32))
        bank = [psum[:, i, :] for i in range(8)]

        def wait_scatter(eng, s, count):
            if not isinstance(count, int) or count > 0:
                eng.wait_ge(s, count * 16)

        def at(i, n):
            return slice(i, i + n) if isinstance(i, int) else bass.ds(i, n)

        cols, ncols = const_layout()
        const = sb("const", [P, ncols])

        def cst(name):
            return const[:, cols[name][0]:cols[name][1]]

        ident = cst("ident")
        x_sb = sb("x_sb", [P, NT, P])
        xr = sb("xr", [P, NT, ROW])
        side = sb("side", [P, NT, P])
        xnT1 = sb("xnT1", [P, NTOK])
        xn = [sb(f"xn{k}", [P, C, P]) for k in range(2)]
        xT = [sb(f"xT{k}", [P, S]) for k in range(2)]
        st = sb("st", [P, NT, 6])
        mv = sb("mv", [P, NT, 2])
        rstd = sb("rstd", [P, NT])
        rtmp = sb("rtmp", [P, NT])
        rvar = sb("rvar", [P, NT])
        lg = sb("lg", [P, NT, E + 1])
        ident16 = sb("ident16", [P, P], BF16)
        before16 = sb("before16", [P, P], BF16)
        tile_before16 = sb("tile_before16", [P, P], BF16)
        same16 = sb("same16", [P, E], BF16)
        ones16 = sb("ones16", [P, P], BF16)
        mask16 = sb("mask16", [P, P], BF16)

        w_qkvo = sb("w_qkvo", [P, 4, P])
        b_qk = sb("b_qk", [P, 2])
        bv_row = sb("bv_row", [P, P])
        bo_row = sb("bo_row", [P, P])
        w_gate0 = sb("w_gate0", [P, E + 1])
        w_sgu = sb("w_sgu", [P, 2, SJ, P])
        w_sd = sb("w_sd", [P, SJ, P])
        w_gu0 = sb("w_gu0", [P, E, 2 * I0])
        w_dn0 = sb("w_dn0", [P, E, 2, P])
        w_q1 = sb("w_q1", [P, H1 * P])
        b_q1 = sb("b_q1", [P, H1])
        w_kv1 = sb("w_kv1", [P, 2 * P])
        b_kv1 = sb("b_kv1", [P, 2])
        w_o1 = sb("w_o1", [P, H1, P])
        w_red1 = sb("w_red1", [P, GD])
        wg1 = sb("wg1", [E, GD])
        wg1s = sb("wg1s", [E, GD])
        wgn = sb("wgn", [E, 3])
        wgT = sb("wgT", [GD, E])

        HG = 4

        class Region:

            def __init__(self, name, words):
                self.memory, self.words, self.used = sb(name, [P, words]), words, {}

            def take(self, user, shape, dt=F32, partitions=P):
                words = 1
                for n in shape:
                    words *= n
                words = words * mybir.dt.size(dt) // 4
                at = self.used.get(user, 0)
                self.used[user] = at + words
                assert at + words <= self.words, (user, at + words)
                flat = self.memory[0:partitions, at:at + words]
                if dt != F32:
                    flat = flat.bitcast(dt)
                names = "abcd"[:len(shape)]
                return flat.rearrange(f"p ({' '.join(names)}) -> p {' '.join(names)}", **dict(zip(names, shape)))

        arena = Region("arena", 16384)
        bench = Region("bench", 8960)
        region = arena.take
        v0 = bench.take("prepare", [NT, H0, VC])

        stQ = [region("attention", [H0, S], BF16) for k in range(2)]
        stK = [region("attention", [H0, S], BF16) for k in range(2)]

        w_up1 = region("weights", [E, HID1])
        w_dn1 = region("weights", [4, E, P])
        b_up1 = region("weights", [E, HID1])
        b_dn1 = region("weights", [E, P])

        qk_scr = nc.dram_tensor("qk_scr", [B, 2, SROW, H0 * S], BF16, kind="Internal").ap()
        slots = [nc.dram_tensor(f"slots{n}", [t * P, ROW], F32, kind="Internal").ap() for n, t in ((0, T0), (1, T1))]
        ys = [nc.dram_tensor(f"ys{n}", [DUMP + T0 * P, P], F32, kind="Internal").ap() for n in range(2)]

        parts = {n: [] for n in ("sync", "scalar", "vector", "gpsimd", "tensor")}

        def on(engine):
            def add(f):
                parts[engine].append(f)
                return f
            return add

        class Chain:

            def __init__(self, name):
                self.sem, self.base, self.n = sem(name), 0, 0

            def inc(self, ins):
                ins.then_inc(self.sem, 1)
                self.n += 1
                return ins

            def sync(self, eng):
                wait(eng, self.sem, self.base + self.n)

            def link(self, eng, ins):
                self.inc(ins)
                self.sync(eng)

            def loop(self, eng, count, k, body):
                start = self.base + self.n
                with eng.Fori(0, count) as i:
                    self.base, self.n = start + i * k, 0
                    body(i)
                    assert self.n == k, (self.n, k)
                self.base, self.n = start + count * k, 0

        dve = Chain("c_dve")
        pool = Chain("c_pool")

        def pairs(eng, chain, k, step, peel=0, first=True):
            for b in range(2 * peel if first else 0):
                step(b, b % 2, b // 2)

            def body(i):
                half = i + peel
                step(half * 2, 0, half)
                step(half * 2 + 1, 1, half)
            if chain is None:
                with eng.Fori(0, B // 2 - 1 - peel) as i:
                    body(i)
            else:
                chain.loop(eng, B // 2 - 1 - peel, k, body)
            step(B - 2, 0, B // 2 - 1)
            step(B - 1, 1, B // 2 - 1)

        def is_last(b):
            return isinstance(b, int) and b == B - 1

        s_x = [sem(f"s_xin{n}") for n in range(4)]
        s_wg1 = sem("s_wg1")
        s_const = sem("s_const")
        s_w0 = sem("s_w0")
        s_shared = sem("s_shared")
        s_pads = sem("s_pads")
        s_exp0 = sem("s_exp0")
        s_w1 = sem("s_w1")
        s_exp1 = sem("s_exp1")

        def row_bcast(v):
            return v.rearrange("(o n) -> o n", o=1).broadcast_to([P, v.shape[0]])

        @on("sync")
        def _(sp):
            sp.dma_start(wg1[:, :], a["wg1"]).then_inc(s_wg1, 16)
            for n in range(4):
                rows = slice(4 * n, 4 * n + 4)
                sp.dma_start(x_sb[:, rows, :], a["x"].rearrange("(i p) d -> p i d", p=P)[:, rows, :]).then_inc(s_x[n], 16)
            sp.dma_start(const[:, :], a["const"]).then_inc(s_const, 16)
            for n, name in enumerate(("Wq0", "Wk0", "Wv0", "Wo0")):
                sp.dma_start(w_qkvo[:, n, :], a[name]).then_inc(s_w0, 16)
            for n, name in enumerate(("bq0", "bk0")):
                sp.dma_start(b_qk[:, n:n + 1], a[name].rearrange("(p o) -> p o", o=1)).then_inc(s_w0, 16)
            sp.dma_start(bv_row[:, :], row_bcast(a["bv0"])).then_inc(s_w0, 16)
            sp.dma_start(bo_row[:, :], row_bcast(a["bo0"])).then_inc(s_w0, 16)
            sp.dma_start(w_gate0[:, :], a["gate0"]).then_inc(s_w0, 16)
            wait(sp, s_pads, 1)
            for n, name in enumerate(("sgate", "sup")):
                sp.dma_start(w_sgu[:, n, :, :].rearrange("p j n -> p (j n)")[:, 0:SI], a[name]).then_inc(s_shared, 16)
            sp.dma_start(w_sd[:, 0:2, :], a["sdown"][0:2 * P, :].rearrange("(j p) n -> p j n", p=P)).then_inc(s_shared, 16)
            sp.dma_start(w_sd[0:SI - 2 * P, 2, :], a["sdown"][2 * P:SI, :]).then_inc(s_shared, 16)
        N_W0, N_SHARED, N_EXP0 = 9, 4, 3

        N_W1, N_EXP1 = 6, 4 * E

        s_var = sem("s_var")
        s_std = sem("s_std")

        def layer_stats(n, arrive):
            @on("vector")
            def _(v):
                for piece in range(4):
                    arrive(v, piece)
                    rows = range(piece * NT // 4, (piece + 1) * NT // 4)
                    for i in rows:
                        dve.inc(v.bn_stats(st[:, i, :], x_sb[:, i, :]))
                    dve.sync(v)
                    for i in rows:
                        dve.inc(v.bn_aggr(mv[:, i, :], st[:, i, :]))
                dve.sync(v)
                v.tensor_scalar(rvar[:, :], mv[:, :, 1], EPS_LN, None, ALU.add).then_inc(s_var, 1)
                wait(v, s_std, n + 1)
                dve.link(v, v.reciprocal(rstd[:, :], rtmp[:, :]))
                wait(v, s_var, n + 1)
                dve.link(v, v.tensor_tensor(rtmp[:, :], rvar[:, :], rstd[:, :], ALU.mult))
                dve.link(v, v.tensor_tensor(rtmp[:, :], rtmp[:, :], rstd[:, :], ALU.mult))
                dve.link(v, v.tensor_scalar(rtmp[:, :], rtmp[:, :], -0.5, 1.5, ALU.mult, ALU.add))
                dve.link(v, v.tensor_tensor(rstd[:, :], rstd[:, :], rtmp[:, :], ALU.mult))

            @on("scalar")
            def _(s):
                wait(s, s_var, n + 1)
                s.activation(rtmp[:, :], rvar[:, :], ACT.Sqrt).then_inc(s_std, 1)

        def normalise(v, b, k, dst_free):
            for c in range(C):
                i = b * C + c
                ins = v.tensor_scalar(xn[k][:, c, :], x_sb[:, i, :], mv[:, i, 0:1], rstd[:, at(i, 1)],
                                      ALU.subtract, ALU.mult)
            ins.then_inc(dst_free, 1)

        s_c16 = sem("s_c16")
        s_slot_init = sem("s_slot_init")
        s_pad_rows = sem("s_pad_rows")
        s_fixed_out = sem("s_fixed_out")
        s_fixed = sem("s_fixed")
        s_stack0 = sem("s_stack0")
        arena.take("padding", [2 * 2 * H0 * S // 2])
        pad_rows = arena.take("padding", [T0, ROW])
        FW = 3 * H0 * S // P
        fixed = [bench.take("prepare", [FW], BF16) for z in range(2)]

        @on("gpsimd")
        def _(g):
            pool.inc(g.memset(w_sgu[:, :, 2, :], 0.0))
            g.memset(w_sd[:, 2, :], 0.0)
            pool.inc(g.memset(w_dn0[:, :, 1, :], 0.0))
            pool.sync(g)
            g.memset(ones16[:, :], 1.0).then_inc(s_pads, 1)
            g.memset(fixed[0][:, :], 0.0).then_inc(s_fixed, 1)
            g.memset(fixed[1][:, :], -1.0).then_inc(s_fixed, 1)
            g.memset(te[:, :].bitcast(F32), 0.0).then_inc(s_c16, 1)
            g.memset(v0[:, :, :, D0:VC], 1.0).then_inc(s_c16, 1)
            wait_dma(g, s_const, 1)
            g.tensor_copy(before16[:, :], cst("before"))
            g.tensor_copy(tile_before16[:, :], cst("tile_before"))
            g.tensor_copy(same16[:, :], cst("same_expert"))
            g.tensor_copy(ident16[:, :], ident)
            g.tensor_copy(mask16[:, :], cst("mask")).then_inc(s_c16, 1)
            for k in range(2):
                g.memset(stQ[k][:, :, :].rearrange("p h s -> p (h s)").bitcast(F32), 0.0).then_inc(s_stack0, 1)
                g.memset(stK[k][:, :, :].rearrange("p h s -> p (h s)").bitcast(F32), 0.0).then_inc(s_stack0, 1)
            pool.link(g, g.memset(pad_rows[:, :, :], 0.0))
            g.tensor_copy(pad_rows[:, :, ROW - 1], cst("dump")).then_inc(s_pad_rows, 1)

        @on("sync")
        def _(sp):
            wait(sp, s_fixed, 2)
            for z in range(2):
                rows = qk_scr[:, z, MROW:SROW, :].rearrange("b t n -> b (t n)").rearrange("b (p n) -> p b n", p=P)
                sp.dma_start(rows, fixed[z][:, :].unsqueeze(1).broadcast_to([P, B, FW])).then_inc(s_fixed_out, 16)
        N_INIT = 2

        s_xn = sem("s_xn")
        s_xr = sem("s_xr")
        s_tx = sem("s_tx")
        s_xT = sem("s_xT")
        s_qk = sem("s_qk")
        s_q32 = sem("s_q32")
        s_qh = sem("s_qh")
        s_r1 = sem("s_r1")
        s_qm = sem("s_qm")
        s_ql = sem("s_ql")
        s_qst = [sem(f"s_qst{k}") for k in range(2)]
        s_v = sem("s_v")
        s_vp = sem("s_vp")
        s_wg = sem("s_wg")
        s_wgt = sem("s_wgt")
        s_g = sem("s_g")
        s_sg = sem("s_sg")
        s_hs = sem("s_hs")
        s_dn = sem("s_dn")
        s_sh = sem("s_sh")
        B_T, B_QK, B_V, B_D = bank[0], bank[1], bank[2], bank[3]
        B_G = bank[4:7]
        qk32 = bench.take("prepare", [2 * S])
        qkr = bench.take("prepare", [2 * S])
        qp = [bench.take("prepare", [3, 2 * S], BF16) for k in range(2)]
        silu_s = [bench.take("prepare", [S]) for j in range(SJ)]
        hid_s = [bench.take("prepare", [SJ, S]) for k in range(2)]

        @on("vector")
        def _(v):
            wait_dma(v, s_wg1, 1)
            dve.link(v, v.tensor_tensor(wg1s[:, :], wg1[:, :], wg1[:, :], ALU.mult))
            dve.link(v, v.tensor_reduce(wgn[:, 0:1], wg1s[:, :], AX.X, ALU.add))
            v.tensor_scalar(wgn[:, 0:1], wgn[:, 0:1], EPS_NORM * EPS_NORM, None, ALU.max).then_inc(s_wg, 1)
            wait(v, s_wg, 2)
            dve.link(v, v.reciprocal(wgn[:, 1:2], wgn[:, 1:2]))
            for a_, b_ in ((0, 1), (2, 1)):
                dve.link(v, v.tensor_tensor(wgn[:, 2:3], wgn[:, a_:a_ + 1], wgn[:, b_:b_ + 1], ALU.mult))
            dve.link(v, v.tensor_scalar(wgn[:, 2:3], wgn[:, 2:3], -0.5, 1.5, ALU.mult, ALU.add))
            dve.link(v, v.tensor_tensor(wgn[:, 1:2], wgn[:, 1:2], wgn[:, 2:3], ALU.mult))
            v.tensor_scalar(wg1s[:, :], wg1[:, :], wgn[:, 1:2], None, ALU.mult).then_inc(s_wg, 1)

        @on("scalar")
        def _(s):
            wait(s, s_wg, 1)
            s.activation(wgn[:, 1:2], wgn[:, 0:1], ACT.Sqrt).then_inc(s_wg, 1)


        layer_stats(0, lambda v, piece: wait_dma(v, s_x[piece], 1))

        @on("vector")
        def _(v):
            normalise(v, 0, 0, s_xn)
            wait(v, s_wgt, 1)
            v.tensor_copy(wgT[:, :], B_D[0:GD, 0:E]).then_inc(s_wg, 1)
            wait_dma(v, s_w0, N_W0)

            def step(b, k, half):
                if not is_last(b):
                    wait(v, s_tx, b)
                    wait(v, s_xr, b)
                    normalise(v, b + 1, 1 - k, s_xn)
                wait(v, s_qk, b + 1)
                wait(v, s_ql, b)
                for n in range(2):
                    ins = v.tensor_scalar(qk32[:, n * S:(n + 1) * S], B_QK[:, n * S:(n + 1) * S], b_qk[:, n:n + 1],
                                          None, ALU.add)
                ins.then_inc(s_q32, 1)
                wait(v, s_v, b + 1)
                tiles = at(b * C, C)
                for c in range(C):
                    v.tensor_tensor(v0[:, b * C + c, :, 0:D0], B_V[:, c * P:(c + 1) * P].rearrange("p (h d) -> p h d", d=D0),
                                    bv_row[:, :].rearrange("p (h d) -> p h d", d=D0), ALU.add)
                v.tensor_copy(lg[:, tiles, :],
                              B_V[:, S:S + C * (E + 1)].rearrange("p (c e) -> p c e", c=C)).then_inc(s_vp, 1)
                hidden(v, b, k, 0)
                wait(v, s_qh, b + 1)
                v.tensor_tensor(qkr[:, :], qk32[:, :], qp[k][:, 0, :], ALU.subtract).then_inc(s_r1, 1)
                hidden(v, b, k, 1)
                wait(v, s_qm, b + 1)
                v.tensor_tensor(qp[k][:, 2, :], qkr[:, :], qp[k][:, 1, :], ALU.subtract).then_inc(s_ql, 1)
                if not (isinstance(b, int) and b == 0):
                    shared(b - 1)
                hidden(v, b, k, 2)

            def shared(b):
                wait(v, s_dn, b + 1)
                v.tensor_copy(side[:, at(b * C, C), :], B_D[:, 0:S].rearrange("p (c n) -> p c n", c=C)).then_inc(s_sh, 1)

            def hidden(v, b, k, j):
                if j == 0:
                    wait(v, s_dn, b - 1)
                wait(v, s_sg, b * SJ + j + 1)
                v.tensor_tensor(hid_s[k][:, j, :], silu_s[j][:, :], B_G[j][:, S:2 * S], ALU.mult).then_inc(s_hs, 1)

            pairs(v, None, 0, step, peel=1)
            shared(B - 1)

        @on("gpsimd")
        def _(g):
            def step(b, k, half):
                wait(g, s_xn, b + 1)
                tiles = at(b * C, C)
                g.tensor_copy(xr[:, tiles, 0:P], xn[k][:, :, :]).then_inc(s_xr, 1)
            pairs(g, None, 0, step)

        @on("scalar")
        def _(s):
            def evacuate_xT(b, k):
                wait(s, s_tx, b + 1)
                wait(s, s_g, (b - 1) * SJ)
                s.copy(xT[k][:, :], B_T[:, 0:S]).then_inc(s_xT, 1)
            evacuate_xT(0, 0)

            def silu(b, k, j):
                wait(s, s_g, b * SJ + j + 1)
                wait(s, s_hs, (b - 1) * SJ + j + 1)
                s.activation(silu_s[j][:, :], B_G[j][:, 0:S], ACT.Silu).then_inc(s_sg, 1)

            def step(b, k, half):
                silu(b, k, 0)
                wait(s, s_q32, b + 1)
                wait_dma(s, s_qst[k], half * NP0)
                s.copy(qp[k][:, 0, :], qk32[:, :]).then_inc(s_qh, 1)
                if not is_last(b):
                    evacuate_xT(b + 1, 1 - k)
                wait(s, s_r1, b + 1)
                s.copy(qp[k][:, 1, :], qkr[:, :]).then_inc(s_qm, 1)
                silu(b, k, 1)
                silu(b, k, 2)
            pairs(s, None, 0, step)

        @on("tensor")
        def _(t):
            wait_dma(t, s_const, 1)
            wait(t, s_wg, 3)
            t.transpose(B_D[0:GD, 0:E], wg1s[:, :], ident[0:E, 0:E]).then_inc(s_wgt, 1)

            def transpose_x(b, k):
                wait(t, s_xn, b + 1)
                wait(t, s_xT, b)
                for c in range(C):
                    mm = t.transpose(B_T[:, c * P:(c + 1) * P], xn[k][:, c, :], ident)
                mm.then_inc(s_tx, 1)
            transpose_x(0, 0)
            wait_dma(t, s_w0, N_W0)
            wait_dma(t, s_shared, N_SHARED)

            def step(b, k, half):
                wait(t, s_xT, b + 1)
                wait(t, s_q32, b)
                for n in range(2):
                    mm = t.matmul(B_QK[:, n * S:(n + 1) * S], w_qkvo[:, n, :], xT[k][:, :], start=True, stop=True)
                mm.then_inc(s_qk, 1)
                wait(t, s_vp, b)
                for c in range(C):
                    x_c = xT[k][:, c * P:(c + 1) * P]
                    t.matmul(B_V[:, c * P:(c + 1) * P], x_c, w_qkvo[:, 2, :], start=True, stop=True)
                    mm = t.matmul(B_V[:, S + c * (E + 1):S + (c + 1) * (E + 1)], x_c, w_gate0[:, :], start=True, stop=True)
                mm.then_inc(s_v, 1)
                gate_up(b, k, 0)
                if not is_last(b):
                    transpose_x(b + 1, 1 - k)
                gate_up(b, k, 1)
                if not (isinstance(b, int) and b == 0):
                    down(b - 1, 1 - k)
                gate_up(b, k, 2)

            def gate_up(b, k, j):
                wait(t, s_hs, (b - 1) * SJ + j + 1)
                for u in range(2):
                    mm = t.matmul(B_G[j][:, u * S:(u + 1) * S], w_sgu[:, u, j, :], xT[k][:, :], start=True, stop=True)
                mm.then_inc(s_g, 1)

            def down(b, k):
                wait(t, s_hs, (b + 1) * SJ)
                wait(t, s_sh, b)
                for c in range(C):
                    for j in range(SJ):
                        mm = t.matmul(B_D[:, c * P:(c + 1) * P], hid_s[k][:, j, c * P:(c + 1) * P], w_sd[:, j, :],
                                      start=(j == 0), stop=(j == SJ - 1))
                mm.then_inc(s_dn, 1)
            pairs(t, None, 0, step, peel=1)
            down(B - 1, 1)

        @on("sync")
        def _(sp):
            def step(b, k, half):
                for part, ready in enumerate((s_qh, s_qm, s_ql)):
                    wait(sp, ready, b + 1)
                    for gq, gk in PAIRS[part]:
                        place = qk_scr[b, 0, gq * D0:(gq + 1) * D0, :].rearrange("d (h s) -> (d h) s", h=H0)
                        both = bass.AP(tensor=place.tensor, offset=place.offset,
                                       ap=[place.ap[0], [(SROW + (gk - gq) * D0) * H0 * S, 2], place.ap[1]])
                        sp.dma_start(both, qp[k][:, part, :].rearrange("p (z s) -> p z s", z=2)).then_inc(s_qst[k], 16)
            for b in range(2):
                step(b, b, 0)
            wait(sp, s_pad_rows, 1)
            for dst, t in ((slots[0], T0), (slots[1], T1)):
                sp.dma_start(dst.rearrange("(p t) r -> p (t r)", p=P),
                             pad_rows[:, 0:t, :].rearrange("p t r -> p (t r)")).then_inc(s_slot_init, 16)
            pairs(sp, None, 0, step, peel=1, first=False)

        def late_loads(sp):
            sp.dma_start(w_gu0[:, :, :], a["gu0"]).then_inc(s_exp0, 16)
            sp.dma_start(w_dn0[:, :, 0, :], a["down0"][:, 0:P, :].rearrange("e i n -> i e n")).then_inc(s_exp0, 16)
            sp.dma_start(w_dn0[0:I0 - P, :, 1, :], a["down0"][:, P:I0, :].rearrange("e i n -> i e n")).then_inc(s_exp0, 16)
            for dst, name in ((w_q1[:, :], "Wq1"), (w_kv1[:, :], "Wkv1"), (w_red1[:, :], "red1")):
                sp.dma_start(dst, a[name]).then_inc(s_w1, 16)
            with nc.allow_non_contiguous_dma(reason="a few bias columns"):
                sp.dma_start(b_q1[:, :], a["bq1"].rearrange("(h p) -> p h", p=P)).then_inc(s_w1, 16)
                sp.dma_start(b_kv1[:, :], a["bkv1"].rearrange("(h p) -> p h", p=P)).then_inc(s_w1, 16)
            sp.dma_start(w_o1[:, :, :], a["Wo1"].rearrange("(h p) n -> p h n", p=P)).then_inc(s_w1, 16)

        s_ex = sem("s_gate_exp")
        s_picked = sem("s_picked")
        s_ranked = sem("s_ranked")
        s_rank = sem("s_rank")
        s_route = sem("s_route")
        gates = sb("gates", [P, NT, E])
        g2 = sb("g2", [P, NT, E])
        pick = [sb(f"pick{n}", [P, NT, E]) for n in range(K0)]
        both16 = sb("both16", [P, NT, E], BF16)
        tot16 = sb("tot16", [P, P], BF16)
        gm = sb("gm", [P, NT])
        wk = sb("wk", [P, K0, NT])
        cand = sb("cand", [P, NT, E])
        counts = sb("counts", [P, E])
        ntile = sb("ntile", [P, E])
        cum = sb("cum", [P, E])
        start_ = sb("start_", [P, E])
        stepcmp = sb("stepcmp", [P, E, NT])
        tilecmp = sb("tilecmp", [P, T0, E - 1])
        tef = sb("tef", [P, T0])
        te = sb("te", [P, T0 + 12], I32)
        rank = sb("rank", [P, NT, E])
        posf = sb("posf", [P, NT])
        pos = sb("pos", [P, K0, NT], U32)
        sig = sb("sig", [P, NT])

        def routing(n, picks, T):
            B_TOT, B_RANK, B_CNT = bank[7][:, 0:P], bank[7][:, P:2 * P], bank[7][:, 2 * P:2 * P + E]

            def per_tile(ap):
                return ap.unsqueeze(2).broadcast_to([P, NT, E])

            def per_expert(ap):
                return ap.unsqueeze(1).broadcast_to([P, NT, E])

            def vector_steps(v):
                def link(ins):
                    dve.inc(ins)

                if n == 0:
                    wait(v, s_sh, B)
                logits = lg[:, :, 0:E]
                wait(v, s_vp if n == 0 else s_lg, B)
                link(v.tensor_reduce(gm[:, :], logits, AX.X, ALU.max))
                yield
                dve.sync(v)
                v.tensor_tensor(gates[:, :, :], logits, per_tile(gm[:, :]), ALU.subtract).then_inc(s_ex, 1)
                yield
                yield
                wait(v, s_ex, 2 + 2 * n)
                if n == 0:
                    link(v.tensor_scalar(sig[:, :], sig[:, :], 1.0, None, ALU.add))
                link(v.tensor_reduce(gm[:, :], gates[:, :, :], AX.X, ALU.add))
                yield
                dve.sync(v)
                link(v.reciprocal(gm[:, :], gm[:, :]))
                if n == 0:
                    link(v.reciprocal(sig[:, :], sig[:, :]))
                yield
                dve.sync(v)
                link(v.tensor_tensor(gates[:, :, :], gates[:, :, :], per_tile(gm[:, :]), ALU.mult))
                src = gates
                for j in range(picks):
                    yield
                    dve.sync(v)
                    link(v.tensor_reduce(wk[:, j, :], src[:, :, :], AX.X, ALU.max))
                    yield
                    dve.sync(v)
                    link(v.tensor_tensor(cand[:, :, :], src[:, :, :], per_tile(wk[:, j, :]), ALU.is_equal))
                    yield
                    dve.sync(v)
                    link(v.tensor_tensor(cand[:, :, :], cand[:, :, :], per_expert(cst("first")), ALU.mult))
                    yield
                    dve.sync(v)
                    link(v.tensor_reduce(gm[:, :], cand[:, :, :], AX.X, ALU.max))
                    yield
                    dve.sync(v)
                    link(v.tensor_tensor(pick[j][:, :, :], cand[:, :, :], per_tile(gm[:, :]), ALU.is_equal))
                    if j + 1 < picks:
                        yield
                        dve.sync(v)
                        link(v.scalar_tensor_tensor(out=g2[:, :, :], in0=pick[j][:, :, :], scalar=-2.0,
                                                    in1=gates[:, :, :], op0=ALU.mult, op1=ALU.add))
                        src = g2
                yield
                dve.sync(v)
                if picks == 2:
                    ins = v.tensor_tensor(both16[:, :, :], pick[0][:, :, :], pick[1][:, :, :], ALU.add)
                else:
                    ins = v.tensor_copy(both16[:, :, :], pick[0][:, :, :])
                ins.then_inc(s_picked, 1)
                yield "picked"
                wait(v, s_ranked, 1 + 2 * n)
                v.tensor_copy(tot16[:, :], B_TOT).then_inc(s_picked, 1)
                yield "totals"
                wait(v, s_ranked, 2 + 2 * n)
                link(v.tensor_copy(counts[:, :], B_CNT))
                v.tensor_copy(rank[:, :, :], B_RANK.rearrange("p (i e) -> p i e", e=E)).then_inc(s_rank, 1)
                yield "ranked"
                dve.sync(v)
                link(v.tensor_tensor(stepcmp[:, :, :], counts[:, :].unsqueeze(2).broadcast_to([P, E, NT]),
                                     cst("steps").unsqueeze(1).broadcast_to([P, E, NT]), ALU.is_gt))
                yield
                dve.sync(v)
                link(v.tensor_reduce(ntile[:, :], stepcmp[:, :, :], AX.X, ALU.add))
                link(v.memset(start_[:, :], 1.0))
                yield
                dve.sync(v)
                link(v.tensor_tensor_scan(cum[:, :], start_[:, :], ntile[:, :], 0.0, ALU.mult, ALU.add))
                yield
                dve.sync(v)
                link(v.tensor_tensor(start_[:, :], cum[:, :], ntile[:, :], ALU.subtract))
                link(v.tensor_tensor(tilecmp[:, 0:T, :],
                                     cst("tiles")[:, 0:T].unsqueeze(2).broadcast_to([P, T, E - 1]),
                                     cum[:, 0:E - 1].unsqueeze(1).broadcast_to([P, T, E - 1]), ALU.is_ge))
                yield
                dve.sync(v)
                link(v.tensor_scalar(start_[:, :], start_[:, :], float(P), None, ALU.mult))
                link(v.tensor_reduce(tef[:, 0:T], tilecmp[:, 0:T, :], AX.X, ALU.add))
                yield
                dve.sync(v)
                wait(v, s_rank, n + 1)
                link(v.tensor_tensor(g2[:, :, :], rank[:, :, :], per_expert(start_[:, :]), ALU.add))
                link(v.tensor_copy(te[:, 2:T + 2], tef[:, 0:T]))
                for j in range(picks):
                    yield
                    dve.sync(v)
                    link(v.tensor_tensor(cand[:, :, :], g2[:, :, :], pick[j][:, :, :], ALU.mult))
                    yield
                    dve.sync(v)
                    link(v.tensor_reduce(posf[:, :], cand[:, :, :], AX.X, ALU.add))
                    yield
                    dve.sync(v)
                    link(v.tensor_copy(pos[:, j, :], posf[:, :]))
                yield
                dve.sync(v)
                v.sem_inc(s_route, 1)

            @on("scalar")
            def _(s):
                wait(s, s_ex, 1 + 2 * n)
                if n == 0:
                    s.activation(sig[:, :], lg[:, :, E], ACT.Exp, scale=-1.0)
                s.activation(gates[:, :, :], gates[:, :, :], ACT.Exp).then_inc(s_ex, 1)

            def tensor_steps(t):
                wait(t, s_picked, 1 + 2 * n)
                flat = both16[:, :, :].rearrange("p i e -> p (i e)")
                t.matmul(B_TOT, flat, ones16[:, :], start=True, stop=True).then_inc(s_ranked, 1)
                yield
                wait(t, s_picked, 2 + 2 * n)
                t.matmul(B_RANK, before16[:, :], flat, start=True, stop=False)
                t.matmul(B_RANK, tot16[:, :], tile_before16[:, :], start=False, stop=True)
                t.matmul(B_CNT, tot16[:, :], same16[:, :], start=True, stop=True).then_inc(s_ranked, 1)
                yield
                wait(t, s_rank, n + 1)

            def scatter(g):
                wait(g, s_route, n + 1)
                wait_dma(g, s_slot_init, N_INIT)
                for j in range(picks):
                    if j:
                        wait_scatter(g, s_scat[n], NT * j)
                    pool.inc(g.tensor_copy(xr[:, :, P], wk[:, j, :]))
                    pool.inc(g.tensor_copy(xr[:, :, P + 1].bitcast(U32), cst("token")[:, j * NT:(j + 1) * NT].bitcast(U32)))
                    pool.sync(g)
                    for i in range(NT):
                        g.indirect_dma_start(out=slots[n], out_offset=bass.IndirectOffsetOnAxis(ap=pos[:, j, i:i + 1], axis=0),
                                             in_=xr[:, i, :], in_offset=None).then_inc(s_scat[n], 16)
            return vector_steps, tensor_steps, scatter

        s_scat = [sem(f"s_scat{n}", software_dma=True) for n in range(2)]
        s_lg = sem("s_lg")
        route0_dve, route0_pe, route0_scatter = routing(0, K0, T0)

        s_stk = [[sem(f"s_stk{part}{k}") for k in range(2)] for part in range(2)]
        s_m = [sem(f"s_m{k}") for k in range(2)]
        s_s1 = sem("s_s1")
        s_mx = sem("s_mx")
        s_mt = sem("s_mt")
        s_mp = sem("s_mp")
        s_s2 = sem("s_s2")
        s_p = sem("s_p")
        s_pv = sem("s_pv")
        s_oq = sem("s_oq")
        s_tok = sem("s_tok")
        s_on = sem("s_on")
        s_ot = sem("s_ot")
        s_oT = sem("s_oT")
        s_wo = sem("s_wo")
        s_x1 = sem("s_x1")
        s_pvz = sem("s_pvz")
        s_v0 = sem("s_v0")
        NG = H0 // HG
        NU = H0 // 2 * C
        mx = [sb(f"mx{k}", [P, H0, C]) for k in range(2)]
        mr = sb("mr", [C * H0, P])
        mp = sb("mp", [C * H0, 3, P], BF16)
        p32 = [[region("attention", [HG, S]) for c in range(C)] for g in range(2)]
        v_row = [region("attention", [C, H0, VC]) for k in range(2)]
        oq = [region("attention", [2, S]) for hf in range(2)]
        den = sb("den", [P, C, 2 * HG])
        onorm = sb("onorm", [P, C, P])
        oT = sb("oT", [P, C, P])
        B_S2 = [psum[:, 0:2, :], psum[:, 2:4, :]]
        B_S1 = [bank[4], bank[5]]
        B_PV, B_M = bank[6], bank[7]

        @on("gpsimd")
        def _(g):
            route0_scatter(g)

        @on("sync")
        def _(sp):
            wait(sp, s_stack0, 4)
            wait_dma(sp, s_fixed_out, 2)

            def load(b, k, half, part):
                if isinstance(b, int) and b < 2:
                    wait_dma(sp, s_qst[k], NP0)
                wait(sp, s_s2, (b - 2) * NG * C + (part + 1) * NG // 2 * C)
                for z, stack in enumerate((stQ[k], stK[k])):
                    cols = slice(part * H0 // 2 * S, (part + 1) * H0 // 2 * S)
                    sp.dma_start(stack[0:SROW, :, :].rearrange("p h s -> p (h s)")[:, cols],
                                 qk_scr[b, z][:, cols]).then_inc(s_stk[part][k], 16)

            def maxima(b, k):
                for t in range(3):
                    wait(sp, s_mp, b * 3 + t + 1)
                    sp.dma_start(stQ[k][MROW + t:MROW + t + 1, :, :].rearrange("o h (c s) -> o (h c) s", c=C),
                                 mp[:, t, :]).then_inc(s_m[k], 16)
            for b in range(2):
                for part in range(2):
                    load(b, b, 0, part)
            maxima(0, 0)
            late_loads(sp)
            for k in range(2):
                wait_dma(sp, s_qst[k], B // 2 * NP0)

            def step(b, k, half):
                if is_last(b):
                    return
                more = not (isinstance(b, int) and b + 2 >= B)
                if more:
                    load(b + 2, k, half + 1, 0)
                maxima(b + 1, 1 - k)
                if more:
                    load(b + 2, k, half + 1, 1)
            pairs(sp, None, 0, step)
        N_STK, N_M = 2, 3

        UNITS = ((4, 9), (9, 14), (14, 16))
        EARLY = 4

        def before(b, k):
            return None if isinstance(b, int) and b == 0 else (b - 1, 1 - k)

        @on("tensor")
        def _(t):
            wait(t, s_sh, B)

            def scores_max(b, k, half, u):
                if u % (NU // 2) == 0:
                    wait_dma(t, s_stk[u // (NU // 2)][k], (half + 1) * N_STK)
                wait(t, s_mx, b * NU + u - 1)
                hp, c = divmod(u, C)
                for n in range(2):
                    h = 2 * hp + n
                    mm = t.matmul(B_S1[u % 2][:, n * S:(n + 1) * S], stQ[k][:, h, c * P:(c + 1) * P], stK[k][:, h, :],
                                  start=True, stop=True)
                mm.then_inc(s_s1, 1)

            def turn_maxima(b, k):
                wait(t, s_mx, (b + 1) * NU)
                wait(t, s_x1, b - 1)
                t.transpose(B_M[0:C * H0, 0:P], mx[k][:, :, :].rearrange("p h c -> p (h c)"), ident).then_inc(s_mt, 1)

            def scores(b, k, half, g, c):
                if g == 0 and c == 0:
                    wait_dma(t, s_m[k], (half + 1) * N_M)
                wait(t, s_p, (b * NG + g) * C + c - 1)
                for n in range(HG):
                    h = g * HG + n
                    mm = t.matmul(B_S2[c][:, n // 2, n % 2 * S:(n % 2 + 1) * S], stK[k][:, h, c * P:(c + 1) * P],
                                  stQ[k][:, h, :], start=True, stop=True)
                mm.then_inc(s_s2, 1)

            def values(b, k, g, c):
                wait(t, s_p, (b * NG + g) * C + c + 1)
                if c == 0:
                    wait(t, s_oq, b * NG + g)
                    if g == 0:
                        wait(t, s_v0, b + 1)
                for n in range(HG):
                    mm = t.matmul(B_PV[32 * n:32 * n + VC, 0:S], v_row[k][:, c, g * HG + n, :], p32[g % 2][c][:, n, :],
                                  start=(c == 0), stop=(c == C - 1))
                if c == C - 1:
                    mm.then_inc(s_pv, 1)

            def turn_values(b, hf):
                wait(t, s_oq, b * NG + 2 * hf + 2)
                if hf:
                    wait(t, s_on, 2 * b + 1)
                else:
                    wait(t, s_mp, (b + 2) * 3 if not is_last(b) else B * 3)
                    wait(t, s_x1, b)
                for j in range(2):
                    for c in range(C):
                        mm = t.transpose(B_M[:, c * S + j * P:c * S + (j + 1) * P], oq[hf][:, j, c * P:(c + 1) * P], ident)
                mm.then_inc(s_tok, 1)

            def turn_outputs(b):
                wait(t, s_on, 2 * b + 2)
                for c in range(C):
                    mm = t.transpose(B_M[:, c * P:(c + 1) * P], onorm[:, c, :], ident)
                mm.then_inc(s_ot, 1)

            def project(b):
                wait(t, s_oT, b + 1)
                for c in range(C):
                    mm = t.matmul(B_M[:, c * P:(c + 1) * P], oT[:, c, :], w_qkvo[:, 3, :], start=True, stop=True)
                mm.then_inc(s_wo, 1)

            wait(t, s_pvz, 1)
            def step(b, k, half):
                prev = before(b, k)
                route = route0_pe(t) if isinstance(b, int) and b == 0 else iter(())
                units = iter(range(UNITS[0][0], NU)) if not is_last(b) else iter(())

                def unit():
                    u = next(units, None)
                    if u is not None:
                        scores_max(b + 1, 1 - k, half + k, u)

                def early_unit(u):
                    if not (isinstance(b, int) and b + 2 >= B):
                        scores_max(b + 2, k, half + 1, u)
                scores(b, k, half, 0, 0)
                unit()
                scores(b, k, half, 0, 1)
                unit()
                if prev:
                    values(*prev, 3, 0)
                unit()
                if prev:
                    values(*prev, 3, 1)
                unit()
                if prev:
                    turn_values(prev[0], 1)
                unit()
                scores(b, k, half, 1, 0)
                unit()
                scores(b, k, half, 1, 1)
                unit()
                if prev:
                    turn_outputs(prev[0])
                values(b, k, 0, 0)
                unit()
                values(b, k, 0, 1)
                unit()
                if prev:
                    project(prev[0])
                unit()
                next(route, None)
                scores(b, k, half, 2, 0)
                unit()
                next(route, None)
                scores(b, k, half, 2, 1)
                unit()
                next(route, None)
                if not is_last(b):
                    turn_maxima(b + 1, 1 - k)
                values(b, k, 1, 0)
                values(b, k, 1, 1)
                scores(b, k, half, 3, 0)
                early_unit(0)
                scores(b, k, half, 3, 1)
                early_unit(1)
                values(b, k, 2, 0)
                early_unit(2)
                values(b, k, 2, 1)
                early_unit(3)
                turn_values(b, 0)

            for u in range(NU):
                scores_max(0, 0, 0, u)
            turn_maxima(0, 0)
            for u in range(EARLY):
                scores_max(1, 1, 0, u)
            pairs(t, None, 0, step, peel=1)
            for c in range(C):
                values(B - 1, 1, 3, c)
            turn_values(B - 1, 1)
            turn_outputs(B - 1)
            project(B - 1)

        @on("scalar")
        def _(s):
            def take_values(b, g):
                wait(s, s_pv, b * NG + g + 1)
                if g % 2 == 0:
                    wait(s, s_tok, 2 * b + g // 2 - 1)
                s.copy(oq[g // 2][:, g % 2, :], B_PV[:, 0:S]).then_inc(s_oq, 1)

            def step(b, k, half):
                prev = before(b, k)
                for g in range(NG):
                    for c in range(C):
                        n = (b * NG + g) * C + c
                        wait(s, s_s2, n + 1)
                        wait(s, s_pv, b * NG + g - 1)
                        s.activation(p32[g % 2][c][:, :, :].rearrange("p h s -> p (h s)"),
                                     B_S2[c].rearrange("p n s -> p (n s)"), ACT.Exp, scale=SCALE0).then_inc(s_p, 1)
                    if g:
                        take_values(b, g - 1)
                    elif prev:
                        take_values(prev[0], NG - 1)
                    if g == 1 and not is_last(b):
                        take_v(b + 1, 1 - k)

            def take_v(b, k):
                wait(s, s_pv, (b - 1) * NG)
                s.copy(v_row[k][:, :, :, :], v0[:, at(b * C, C), :, :]).then_inc(s_v0, 1)
            wait_dma(s, s_slot_init, N_INIT)
            wait(s, s_c16, 3)
            wait(s, s_vp, B)
            take_v(0, 0)
            pairs(s, None, 0, step, peel=1)
            take_values(B - 1, NG - 1)

        @on("vector")
        def _(v):
            def maximum(b, k, u):
                hp, c = divmod(u, C)
                wait(v, s_s1, b * NU + u + 1)
                if u == 0:
                    wait(v, s_mt, b - 1)
                v.tensor_reduce(mx[k][:, 2 * hp:2 * hp + 2, c], B_S1[u % 2].rearrange("p (n s) -> p n s", n=2), AX.X,
                                ALU.max).then_inc(s_mx, 1)

            def maxima_parts(b, k, half):
                wait(v, s_mt, b + 1)
                if not (isinstance(b, int) and b == 0):
                    wait_dma(v, s_m[1 - k], (half + k) * N_M)
                m = B_M[0:C * H0, 0:P]
                v.tensor_copy(mp[:, 0, :], m).then_inc(s_mp, 1)
                wait(v, s_mp, 3 * b + 1)
                dve.link(v, v.tensor_tensor(mr[:, :], m, mp[:, 0, :], ALU.subtract))
                v.tensor_copy(mp[:, 1, :], mr[:, :]).then_inc(s_mp, 1)
                wait(v, s_mp, 3 * b + 2)
                v.tensor_tensor(mp[:, 2, :], mr[:, :], mp[:, 1, :], ALU.subtract).then_inc(s_mp, 1)

            def divide(b, hf):
                wait(v, s_tok, 2 * b + hf + 1)
                tok = B_M.rearrange("p (c n q) -> p c n q", c=C, q=32)
                dve.link(v, v.reciprocal(den[:, :, :], tok[:, :, :, D0]))
                if hf == 0:
                    wait(v, s_ot, b)
                half_cols = onorm[:, :, hf * 2 * HG * D0:(hf + 1) * 2 * HG * D0].rearrange("p c (n d) -> p c n d", d=D0)
                v.tensor_tensor(half_cols, tok[:, :, :, 0:D0],
                                den[:, :, :].unsqueeze(3).broadcast_to([P, C, 2 * HG, D0]), ALU.mult).then_inc(s_on, 1)

            def outputs(b):
                wait(v, s_ot, b + 1)
                wait(v, s_wo, b)
                v.tensor_copy(oT[:, :, :].rearrange("p c n -> p (c n)"), B_M[:, 0:C * P]).then_inc(s_oT, 1)

            def add_to_stream(b):
                wait(v, s_wo, b + 1)
                tiles = at(b * C, C)
                v.tensor_tensor(x_sb[:, tiles, :], B_M[:, 0:C * P].rearrange("p (c n) -> p c n", c=C), x_sb[:, tiles, :],
                                ALU.add).then_inc(s_x1, 1)

            v.memset(B_PV, 0.0).then_inc(s_pvz, 1)
            for u in range(NU):
                maximum(0, 0, u)
            maxima_parts(0, 0, 0)
            for u in range(EARLY):
                maximum(1, 1, u)
            wait(v, s_c16, 3)
            route = route0_dve(v)

            def step(b, k, half):
                prev = before(b, k)
                first_row, second_row = (isinstance(b, int) and b == n for n in range(2))
                pieces = iter(lambda: next(route), "picked") if first_row else route if second_row else iter(())

                def unit(u):
                    if not is_last(b):
                        maximum(b + 1, 1 - k, u)
                    for _ in range(2):
                        next(pieces, None)
                for u in range(*UNITS[0]):
                    unit(u)
                if prev:
                    divide(prev[0], 1)
                first, last = UNITS[1]
                for u in range(first, last - 2):
                    unit(u)
                if prev:
                    outputs(prev[0])
                for u in range(last - 2, last):
                    unit(u)
                if prev:
                    add_to_stream(prev[0])
                if first_row:
                    assert next(route) == "totals"
                for u in range(*UNITS[2]):
                    unit(u)
                if first_row:
                    assert next(route) == "ranked"
                if not is_last(b):
                    maxima_parts(b + 1, 1 - k, half + k)
                for u in range(EARLY):
                    if not (isinstance(b, int) and b + 2 >= B):
                        maximum(b + 2, k, u)
                    if first_row:
                        next(route)
                divide(b, 0)

            pairs(v, dve, 2 * 3, step, peel=1)
            assert next(route, None) is None
            divide(B - 1, 1)
            outputs(B - 1)
            add_to_stream(B - 1)

        xs = [sb(f"xs{r}", [P, ROW]) for r in range(4)]
        ends = [sb(f"ends{r}", [P, 2]) for r in range(8)]
        xsT = [sb(f"xsT{k}", [P, P]) for k in range(2)]
        act_t = [sb(f"act_t{k}", [P, HID1]) for k in range(2)]
        hid = [sb(f"hid{k}", [P, HID1]) for k in range(2)]
        hidT = [sb(f"hidT{k}", [P, HID1]) for k in range(2)]
        y = [sb(f"y{r}", [P, P]) for r in range(8)]
        y0 = [sb(f"yb{r}", [P, P]) for r in range(2)]
        names = ("tx", "en", "xT", "up", "ac", "hd", "ht", "hT", "dn", "y")

        def experts(n, T):
            q = {m: sem(f"e{n}_{m}") for m in names}
            q_part = sem(f"e{n}_part")
            q_ld = [sem(f"e{n}_ld{r}") for r in range(4)]
            U = EXPERT_TURN[n]
            q_sc = [sem(f"e{n}_sc{r}", software_dma=True) for r in range(U)]
            KC = 2 if n == 0 else 4
            B_X, B_G2, B_H, B_Y = bank[0:2], bank[2:4], bank[4:6], bank[6:8]

            e = {}
            slot = {}

            def steps(eng, chain, k, step, with_experts=False):
                def run(first, turn, outer, count):
                    if with_experts:
                        loaded = nc.values_load_multi_w_load_instructions(
                            te[0:1, at(first, U + 2)], engines=[eng.engine], min_val=0, max_val=E - 1,
                            skip_runtime_bounds_check_because="an expert is a count of E - 1 comparisons")[1]
                    for place in range(count):
                        if with_experts:
                            e["down"], e["up"] = loaded[place], loaded[place + 2]
                        slot["up"] = place, outer
                        slot["down"] = (place - 2) % U, outer - (place < 2)
                        step(first + place, place % 4, turn + place // 4)

                def body(i):
                    run(i * U + U, i * (U // 4) + U // 4, i + 1, U)
                run(0, 0, 0, U)
                if chain is None:
                    with eng.Fori(0, T // U - 2) as i:
                        body(i)
                else:
                    chain.loop(eng, T // U - 2, k * (U // 4), body)
                run(T - U, (T - U) // 4, T // U - 1, U)
                run(T, T // 4, T // U, 2)

            def ring(r, turn, d):
                return (r + d) % 4, turn + (r + d) // 4

            def has(t):
                return not isinstance(t, int) or 0 <= t < T

            @on("sync")
            def _(sp):
                wait_scatter(sp, s_scat[n], NT * (K0 if n == 0 else 1))

                def load(t, r):
                    if has(t):
                        wait(sp, q["tx"], t - 3)
                        wait(sp, q["en"], t - 3)
                        sp.dma_start(xs[r][:, :], slots[n][at(t * P, P), :]).then_inc(q_ld[r], 16)
                for t in range(4):
                    load(t, t)

                def step(t, r, turn):
                    load(t + 4, r)
                    if n == 0 and r == 0 and beside(turn):
                        e = turn - 1
                        sp.dma_start(w_up1[:, at(e, 1), :],
                                     a["w1"].rearrange("e p n -> p e n")[:, at(e, 1), :]).then_inc(s_exp1, 16)
                        sp.dma_start(w_dn1[:, :, at(e, 1), :].rearrange("p c o n -> p (c o) n"),
                                     a["w2"][at(e, 1), :, :].rearrange("o (c p) n -> p (o c) n", p=P)).then_inc(s_exp1, 16)
                        sp.dma_start(b_up1[:, at(e, 1), :],
                                     a["b1"][at(e, 1), :].broadcast_to([P, HID1]).unsqueeze(1)).then_inc(s_exp1, 16)
                        sp.dma_start(b_dn1[:, at(e, 1), :],
                                     a["b2"][at(e, 1), :].broadcast_to([P, P]).unsqueeze(1)).then_inc(s_exp1, 16)
                if n == 0:
                    wait(sp, s_x1, B)
                steps(sp, None, 0, step)

            @on("tensor")
            def _(pe):
                wait_dma(pe, s_exp0 if n == 0 else s_exp1, N_EXP0 if n == 0 else N_EXP1)
                wait(pe, s_x1 if n == 0 else s_x2, B)

                def turn_x(t, r, turn):
                    if has(t):
                        wait_dma(pe, q_ld[r], turn + 1)
                        wait(pe, q["xT"], t - 1)
                        pe.transpose(B_X[r % 2][:, 0:P], xs[r][:, 0:P], ident).then_inc(q["tx"], 1)

                def step(t, r, turn):
                    turn_x(t + 1, *ring(r, turn, 1))
                    if has(t):
                        k = r % 2
                        wait(pe, q["xT"], t + 1)
                        wait(pe, q["hd"] if n == 0 else q["ac"], t - 1)
                        if n == 0:
                            mm = pe.matmul(B_G2[k][:, 0:2 * I0], xsT[k][:, :], w_gu0[:, e["up"], :], start=True, stop=True)
                        else:
                            mm = pe.matmul(B_G2[k][:, :], xsT[k][:, :], w_up1[:, e["up"], :], start=True, stop=True)
                        mm.then_inc(q["up"], 1)
                    if has(t - 1):
                        k = (r - 1) % 2
                        wait(pe, q["hd"], t)
                        wait(pe, q["hT"], t - 2)
                        for j in range(KC):
                            mm = pe.transpose(B_H[k][:, j * P:(j + 1) * P], hid[k][:, j * P:(j + 1) * P], ident)
                        mm.then_inc(q["ht"], 1)
                    if has(t - 2):
                        k = r % 2
                        wait(pe, q["hT"], t - 1)
                        wait(pe, q["y"], t - 3)
                        for j in range(KC):
                            w = w_dn0[:, e["down"], j, :] if n == 0 else w_dn1[:, j, e["down"], :]
                            mm = pe.matmul(B_Y[k][:, 0:P], hidT[k][:, j * P:(j + 1) * P], w, start=(j == 0), stop=(j == KC - 1))
                        mm.then_inc(q["dn"], 1)
                turn_x(0, 0, 0)
                steps(pe, None, 0, step, with_experts=True)

            @on("scalar")
            def _(s):
                def take_x(t, r):
                    if has(t):
                        wait(s, q["tx"], t + 1)
                        wait(s, q["up"], t - 1)
                        s.copy(xsT[r % 2][:, :], B_X[r % 2][:, 0:P]).then_inc(q["xT"], 1)

                def step(t, r, turn):
                    take_x(t + 1, (r + 1) % 4)
                    if has(t):
                        k = r % 2
                        if n == 0:
                            wait(s, q["up"], t + 1)
                            wait(s, q["hd"], t - 1)
                            s.activation(act_t[k][:, 0:I0], B_G2[k][:, 0:I0], ACT.Silu).then_inc(q["ac"], 1)
                        else:
                            wait(s, q["ac"], t + 1)
                            wait(s, q["ht"], t - 1)
                            s.activation(hid[k][:, :], act_t[k][:, :], ACT.Gelu).then_inc(q["hd"], 1)
                    if has(t - 1):
                        k = (r - 1) % 2
                        wait(s, q["ht"], t)
                        wait(s, q["dn"], t - 2)
                        s.copy(hidT[k][:, 0:KC * P], B_H[k][:, 0:KC * P]).then_inc(q["hT"], 1)
                take_x(0, 0)
                steps(s, None, 0, step)

            @on("vector")
            def _(v):
                wait(v, s_route, n + 1)
                if n == 0:
                    wait(v, s_x1, B)
                    for k in range(2):
                        dve.link(v, v.memset(hid[k][:, I0:2 * P], 0.0))

                def step(t, r, turn):
                    if n == 0 and beside(turn):
                        merge_shared(v, turn - 1, r)
                    if has(t):
                        wait_dma(v, q_ld[r], turn + 1)
                        out, outer = slot["up"]
                        wait_scatter(v, q_sc[out], outer)
                        v.tensor_copy(ends[out][:, :].bitcast(U32), xs[r][:, P:P + 2].bitcast(U32)).then_inc(q["en"], 1)
                        k = r % 2
                        wait(v, q["up"], t + 1)
                        if n == 0:
                            wait(v, q["ac"], t + 1)
                            wait(v, q["ht"], t - 1)
                            v.tensor_tensor(hid[k][:, 0:I0], act_t[k][:, 0:I0], B_G2[k][:, I0:2 * I0],
                                            ALU.mult).then_inc(q["hd"], 1)
                        else:
                            wait(v, q["hd"], t - 1)
                            v.tensor_tensor(act_t[k][:, :], B_G2[k][:, :], b_up1[:, e["up"], :], ALU.add).then_inc(q["ac"], 1)
                    if has(t - 2):
                        out, _ = slot["down"]
                        wait(v, q["dn"], t - 1)
                        wait(v, q["en"], t - 1)
                        src = B_Y[r % 2][:, 0:P]
                        if n:
                            dve.link(v, v.tensor_tensor(y0[r % 2][:, :], src, b_dn1[:, e["down"], :], ALU.add))
                            src = y0[r % 2][:, :]
                        v.tensor_scalar(y[out][:, :], src, ends[out][:, 0:1], None, ALU.mult).then_inc(q["y"], 1)
                steps(v, dve, 4 if n else 2, step, with_experts=(n == 1))

            @on("gpsimd")
            def _(g):
                def step(t, r, turn):
                    if has(t - 2):
                        out, _ = slot["down"]
                        wait(g, q["en"], t - 1)
                        wait(g, q["y"], t - 1)
                        g.sem_inc(q_part, 1)
                        g.indirect_dma_start(out=ys[n], out_offset=bass.IndirectOffsetOnAxis(
                            ap=ends[out][:, 1:2].bitcast(U32), axis=0), in_=y[out][:, :], in_offset=None).then_inc(q_sc[out], 16)
                steps(g, None, 0, step)
            return q_sc

        s_x2 = sem("s_x2")
        s_merged = sem("s_merged")

        def merge_shared(v, turn, r):
            rows = at(turn * 2, 2)
            wide = [P, 2, P]
            if r:
                dve.sync(v)
            if r == 0:
                gate = sig[:, rows].unsqueeze(2).broadcast_to(wide)
                dve.inc(v.tensor_tensor(side[:, rows, :], side[:, rows, :], gate, ALU.mult))
            elif r == 1:
                bias = bo_row[:, :].unsqueeze(1).broadcast_to(wide)
                dve.inc(v.tensor_tensor(side[:, rows, :], side[:, rows, :], bias, ALU.add))
            elif r == 2:
                v.tensor_tensor(x_sb[:, rows, :], x_sb[:, rows, :], side[:, rows, :], ALU.add).then_inc(s_merged, 1)

        def beside(turn):
            return not isinstance(turn, int) or 1 <= turn < T0 // 4 - 1
        assert T0 // 4 - 2 == NT // 2 == E

        s_sc0 = experts(0, T0)

        s_xn1 = sem("s_xn1")
        s_xr1 = sem("s_xr1")
        s_tx1 = sem("s_tx1")
        s_xT1 = sem("s_xT1")
        s_red = sem("s_red")
        s_redT = sem("s_redT")
        s_lgm = sem("s_lgm")
        redT = [bench.take("attention", [S], partitions=GD) for k in range(2)]
        B_T1, B_RED, B_LG = (bank[0], bank[3]), bank[1], bank[2]

        s_side = [[sem(f"s_side{j}{n}") for n in range(4)] for j in range(K0)]
        s_half = sem("s_half")
        out_k = (side[:, :, :], xnT1[:, :].rearrange("p (i d) -> p i d", d=P))
        N4 = NT // 4

        @on("sync")
        def _(sp):
            for q in s_sc0:
                wait_scatter(sp, q, T0 // EXPERT_TURN[0])
            wait(sp, s_merged, T0 // 4 - 2)
            for n in range(4):
                rows = slice(n * N4, (n + 1) * N4)
                for j in range(K0):
                    y_j = ys[0][j * NTOK:(j + 1) * NTOK, :].rearrange("(i p) d -> p i d", p=P)
                    sp.dma_start(out_k[j][:, rows, :], y_j[:, rows, :]).then_inc(s_side[j][n], 16)

        @on("gpsimd")
        def _(g):
            for n in range(4):
                rows = slice(n * N4, (n + 1) * N4)
                wait_dma(g, s_side[0][n], 1)
                g.tensor_tensor(x_sb[:, rows, :], x_sb[:, rows, :], out_k[0][:, rows, :], ALU.add).then_inc(s_half, 1)

        def add_expert_outputs(v, n):
            rows = slice(n * N4, (n + 1) * N4)
            wait_dma(v, s_side[1][n], 1)
            wait(v, s_half, n + 1)
            dve.link(v, v.tensor_tensor(x_sb[:, rows, :], x_sb[:, rows, :], out_k[1][:, rows, :], ALU.add))
        layer_stats(1, add_expert_outputs)

        @on("vector")
        def _(v):
            for b in range(2):
                normalise(v, b, b, s_xn1)

            def take_logits(b):
                wait(v, s_lgm, b + 1)
                v.tensor_copy(lg[:, at(b * C, C), 0:E], B_LG[:, 0:C * E].rearrange("p (c e) -> p c e", c=C)).then_inc(s_lg, 1)

            def step(b, k, half):
                if not (isinstance(b, int) and b + 2 >= B):
                    wait(v, s_tx1, b + 1)
                    wait(v, s_xr1, b + 1)
                    normalise(v, b + 2, k, s_xn1)
                if not (isinstance(b, int) and b == 0):
                    take_logits(b - 1)
            pairs(v, None, 0, step, peel=1)
            take_logits(B - 1)

        @on("gpsimd")
        def _(g):
            wait_scatter(g, s_scat[0], NT * K0)
            def step(b, k, half):
                wait(g, s_xn1, b + 1)
                g.tensor_copy(xr[:, at(b * C, C), 0:P], xn[k][:, :, :]).then_inc(s_xr1, 1)
            pairs(g, None, 0, step)

        @on("scalar")
        def _(s):
            def take_xT(b, k):
                wait(s, s_tx1, b + 1)
                s.copy(xnT1[:, at(b * S, S)], B_T1[k][:, 0:S]).then_inc(s_xT1, 1)
            take_xT(0, 0)

            def step(b, k, half):
                if not is_last(b):
                    take_xT(b + 1, 1 - k)
                wait(s, s_red, b + 1)
                wait(s, s_lgm, b - 1)
                s.copy(redT[k][:, :], B_RED[0:GD, 0:S]).then_inc(s_redT, 1)
            pairs(s, None, 0, step)

        @on("tensor")
        def _(t):
            for q in s_sc0:
                wait_scatter(t, q, T0 // EXPERT_TURN[0])

            def turn(b, k):
                wait(t, s_xn1, b + 1)
                wait(t, s_xT1, b - 1)
                for c in range(C):
                    mm = t.transpose(B_T1[k][:, c * P:(c + 1) * P], xn[k][:, c, :], ident)
                mm.then_inc(s_tx1, 1)
            turn(0, 0)
            wait(t, s_wg, 4)
            wait_dma(t, s_w1, N_W1)

            def logits(b, k):
                wait(t, s_redT, b + 1)
                wait(t, s_lg, b)
                for c in range(C):
                    mm = t.matmul(B_LG[:, c * E:(c + 1) * E], redT[k][:, c * P:(c + 1) * P], wgT[:, :], start=True, stop=True)
                mm.then_inc(s_lgm, 1)

            def step(b, k, half):
                if not is_last(b):
                    turn(b + 1, 1 - k)
                wait(t, s_xT1, b + 1)
                wait(t, s_redT, b)
                t.matmul(B_RED[0:GD, 0:S], w_red1[:, :], xnT1[:, at(b * S, S)], start=True, stop=True).then_inc(s_red, 1)
                if not (isinstance(b, int) and b == 0):
                    logits(b - 1, 1 - k)
            pairs(t, None, 0, step, peel=1)
            logits(B - 1, 1)

        route1_dve, route1_pe, route1_scatter = routing(1, 1, T1)

        s_xb = sem("s_xb")
        s_kv = sem("s_kv")
        s_kT = sem("s_kT")
        s_Q = sem("s_Q")
        s_q = sem("s_q")
        s_S = sem("s_S")
        s_nm = sem("s_nm")
        s_P = sem("s_P")
        s_Pn = sem("s_Pn")
        s_T = sem("s_T")
        s_PT = sem("s_PT")
        s_V = sem("s_V")
        s_o = sem("s_o")
        s_W = sem("s_W")
        LEFT = P + S
        xb = [bench.take("attention", [S]) for k in range(2)]
        kT = [bench.take("attention", [S]) for k in range(2)]
        v1 = [bench.take("attention", [S]) for k in range(2)]
        qT = [bench.take("attention", [S]) for k in range(2)]
        prob = [bench.take("attention", [LEFT]) for r in range(4)]
        probT = [bench.take("attention", [LEFT]) for k in range(2)]
        rowmax = [sb(f"rowmax{k}", [P, C]) for k in range(2)]
        negmax = [sb(f"negmax{r}", [P, C]) for r in range(4)]
        rowsum = [sb(f"rowsum{r}", [P, C]) for r in range(4)]
        oT1 = [bench.take("attention", [H1, S]) for k in range(2)]
        pe_T = cst("pe")
        B_Q, B_O, B_S, B_TT, B_W = bank[0], (bank[1], bank[6]), bank[2:4], bank[4:6], bank[7]
        TURNS = (slice(0, P), slice(P, 2 * P), slice(2 * P, 3 * P))

        def heads(eng, chain, k_links, stages, extra=()):
            def run(b, k, h, upto):
                for lag, f in stages:
                    hh = h - lag
                    bb, kk = (b, k) if 0 <= hh < H1 else (b - 1, 1 - k)
                    if hh >= H1 or (isinstance(bb, int) and bb < 0):
                        continue
                    hh %= H1
                    f(bb, kk, hh, bb * H1 + hh)

            def step(b, k, half):
                for h in range(H1):
                    run(b, k, h, H1)
                    for where, f in extra:
                        if where == h:
                            f(b, k)
            pairs(eng, chain, k_links, step, peel=1)
            for h in range(5):
                for lag, f in stages:
                    hh = H1 + h - lag
                    if hh < H1:
                        f(B - 1, 1, hh, (B - 1) * H1 + hh)

        @on("gpsimd")
        def _(g):
            wait(g, s_xT1, 2)
            for b in range(2):
                g.tensor_copy(xb[b][:, :], xnT1[:, b * S:(b + 1) * S]).then_inc(s_xb, 1)

            def step(b, k, half):
                if not (isinstance(b, int) and b + 2 >= B):
                    wait(g, s_xT1, b + 3)
                    wait(g, s_kv, b + 1)
                    g.tensor_copy(xb[k][:, :], xnT1[:, at((b + 2) * S, S)]).then_inc(s_xb, 1)
            step(0, 0, 0)
            route1_scatter(g)
            step(1, 1, 0)
            pairs(g, None, 0, step, peel=1, first=False)

        @on("tensor")
        def _(t):
            wait(t, s_lg, B)

            def queries(b, k, h, H):
                wait(t, s_q, H)
                t.matmul(B_Q[:, 0:S], w_q1[:, h * P:(h + 1) * P], xnT1[:, at(b * S, S)], start=True, stop=True).then_inc(s_Q, 1)

            def keys_values(b, k):
                wait(t, s_xb, b + 1)
                t.matmul(B_W[:, 0:S], w_kv1[:, 0:P], xb[k][:, :], start=True, stop=True)
                for c in range(C):
                    mm = t.matmul(B_W[:, S + c * P:S + (c + 1) * P], xb[k][:, c * P:(c + 1) * P], w_kv1[:, P:2 * P],
                                  start=True, stop=True)
                mm.then_inc(s_kv, 1)

            def next_keys_values(b, k):
                if not is_last(b):
                    wait(t, s_x2, b)
                    keys_values(b + 1, 1 - k)

            def scores(b, k, h, H):
                wait(t, s_q, H + 1)
                wait(t, s_kT, b + 1)
                wait(t, s_P, H - 1)
                o, q = B_S[h % 2], qT[h % 2]
                t.matmul(o[:, 0:P], q[:, 0:P], kT[k][:, 0:P], start=True, stop=False)
                t.matmul(o[:, 0:P], ident16[:, :], mask16[:, :], start=False, stop=True)
                t.matmul(o[:, P:LEFT], q[:, P:S], kT[k][:, :], start=True, stop=False)
                t.matmul(o[:, 2 * P:LEFT], ident16[:, :], mask16[:, :], start=False, stop=True).then_inc(s_S, 1)

            def turn(b, k, h, H):
                wait(t, s_Pn, H + 1)
                wait(t, s_PT, H - 1)
                for cols in TURNS:
                    mm = t.transpose(B_TT[h % 2][:, cols], prob[h % 4][:, cols], ident)
                mm.then_inc(s_T, 1)

            def values(b, k, h, H):
                wait(t, s_PT, H + 1)
                wait(t, s_o, H - 1)
                pT, o = probT[h % 2], B_O[h % 2]
                t.matmul(o[:, 0:S], v1[k][:, 0:P], pT[:, 0:S], start=True, stop=False)
                t.matmul(o[:, P:S], v1[k][:, P:S], pT[:, S:LEFT], start=False, stop=True).then_inc(s_V, 1)

            def project(b, k):
                wait(t, s_o, (b + 1) * H1)
                wait(t, s_kT, b + 2 if not is_last(b) else B)
                for c in range(C):
                    for h in range(H1):
                        mm = t.matmul(B_W[:, c * P:(c + 1) * P], oT1[k][:, h, c * P:(c + 1) * P], w_o1[:, h, :],
                                      start=(h == 0), stop=(h == H1 - 1))
                mm.then_inc(s_W, 1)

            def last_project(b, k):
                if not isinstance(b, int) or b > 0:
                    project(b - 1, 1 - k)

            route = route1_pe(t)

            def route_step(b, k):
                if isinstance(b, int) and b == 0:
                    next(route, None)

            keys_values(0, 0)
            heads(t, None, 0, ((0, queries), (4, turn), (1, scores), (5, values)),
                  ((4, route_step), (5, route_step), (5, last_project), (7, route_step), (7, next_keys_values)))
            project(B - 1, 1)

        @on("vector")
        def _(v):
            def queries(b, k, h, H):
                wait(v, s_Q, H + 1)
                wait(v, s_S, H - 1)
                v.scalar_tensor_tensor(out=qT[h % 2][:, :], in0=B_Q[:, 0:S], scalar=b_q1[:, h:h + 1], in1=pe_T,
                                       op0=ALU.add, op1=ALU.add).then_inc(s_q, 1)

            def maxima(b, k, h, H):
                wait(v, s_S, H + 1)
                o = B_S[h % 2]
                dve.inc(v.tensor_reduce(rowmax[h % 2][:, 0:1], o[:, 0:P], AX.X, ALU.max))
                dve.link(v, v.tensor_reduce(rowmax[h % 2][:, 1:2], o[:, P:LEFT], AX.X, ALU.max))
                wait(v, s_P, H - 3)
                v.tensor_scalar(negmax[h % 4][:, :], rowmax[h % 2][:, :], -SCALE1, None, ALU.mult).then_inc(s_nm, 1)

            def divide(b, k, h, H):
                wait(v, s_P, H + 1)
                r = h % 4
                dve.link(v, v.reciprocal(rowsum[r][:, :], rowsum[r][:, :]))
                v.tensor_scalar(prob[r][:, 0:P], prob[r][:, 0:P], rowsum[r][:, 0:1], None, ALU.mult)
                v.tensor_scalar(prob[r][:, P:LEFT], prob[r][:, P:LEFT], rowsum[r][:, 1:2], None, ALU.mult).then_inc(s_Pn, 1)

            def take_T(b, k, h, H):
                wait(v, s_T, H + 1)
                wait(v, s_V, H - 1)
                v.tensor_copy(probT[h % 2][:, :], B_TT[h % 2][:, 0:LEFT]).then_inc(s_PT, 1)

            def keys_values(b, k):
                wait(v, s_kv, b + 1)
                v.scalar_tensor_tensor(out=kT[k][:, :], in0=B_W[:, 0:S], scalar=b_kv1[:, 0:1], in1=pe_T,
                                       op0=ALU.add, op1=ALU.add)
                v.tensor_copy(v1[k][:, :], B_W[:, S:2 * S]).then_inc(s_kT, 1)

            def next_keys_values(b, k):
                if not is_last(b):
                    keys_values(b + 1, 1 - k)

            def add_to_stream(b, k):
                wait(v, s_W, b + 1)
                rows = x_sb[:, at(b * C, C), :]
                v.tensor_tensor(rows, B_W[:, 0:S].rearrange("p (c n) -> p c n", c=C), rows, ALU.add).then_inc(s_x2, 1)

            def last_stream(b, k):
                if not isinstance(b, int) or b > 0:
                    add_to_stream(b - 1, 1 - k)

            route = route1_dve(v)
            pace = iter((3, 3, 3, 4, 1, 0, 1, 2) + (2,) * 8)

            def route_steps(b, k):
                if isinstance(b, int) and b <= 1:
                    for _ in range(next(pace)):
                        next(route, None)

            keys_values(0, 0)
            heads(v, dve, 2 * H1 * 3, ((0, queries), (4, take_T), (1, maxima), (2, divide)),
                  ((6, last_stream), (7, next_keys_values)) + tuple((h, route_steps) for h in range(H1)))
            assert next(route, None) is None
            add_to_stream(B - 1, 1)

        @on("scalar")
        def _(s):
            def exponentials(b, k, h, H):
                wait(s, s_nm, H + 1)
                wait(s, s_T, H - 3)
                r = h % 4
                for c, cols in enumerate((slice(0, P), slice(P, LEFT))):
                    ins = s.activation(prob[r][:, cols], B_S[h % 2][:, cols], ACT.Exp, bias=negmax[r][:, c:c + 1],
                                       scale=SCALE1, accum_out=rowsum[r][:, c:c + 1])
                ins.then_inc(s_P, 1)

            def outputs(b, k, h, H):
                wait(s, s_V, H + 1)
                wait(s, s_W, b - 1)
                s.activation(oT1[k][:, h, :], B_O[h % 2][:, 0:S], ACT.Identity, bias=b_kv1[:, 1:2]).then_inc(s_o, 1)
            heads(s, None, 0, ((1, exponentials), (5, outputs)))

        s_sc1 = experts(1, T1)

        s_piece = [sem(f"s_piece{n}") for n in range(4)]
        s_sum = sem("s_sum")
        s_out = [sem(f"s_out{n}") for n in range(4)]

        @on("sync")
        def _(sp):
            for q in s_sc1:
                wait_scatter(sp, q, T1 // EXPERT_TURN[1])
            for n in range(4):
                sp.dma_start(side[:, n * N4:(n + 1) * N4, :],
                             ys[1][n * N4 * P:(n + 1) * N4 * P, :].rearrange("(i p) d -> p i d", p=P)).then_inc(s_piece[n], 16)
            for n in range(4):
                wait(sp, s_sum, n + 1)
                sp.dma_start(out.rearrange("(i p) d -> p i d", p=P)[:, n * N4:(n + 1) * N4, :],
                             x_sb[:, n * N4:(n + 1) * N4, :]).then_inc(s_out[n], 16)
            for n in range(4):
                wait_dma(sp, s_out[n], 1)

        @on("vector")
        def _(v):
            for n in range(4):
                wait_dma(v, s_piece[n], 1)
                rows = slice(n * N4, (n + 1) * N4)
                v.tensor_tensor(x_sb[:, rows, :], x_sb[:, rows, :], side[:, rows, :], ALU.add).then_inc(s_sum, 1)

        block = ctx.enter_context(nc.Block())

        @block.gpsimd
        def _(g):
            for s in sems:
                g.sem_inc(s, CREDIT)
            for f in parts["gpsimd"]:
                f(g)

        @block.sync
        def _(e):
            for f in parts["sync"]:
                f(e)

        @block.scalar
        def _(e):
            for f in parts["scalar"]:
                f(e)

        @block.vector
        def _(e):
            for f in parts["vector"]:
                f(e)

        @block.tensor
        def _(e):
            for f in parts["tensor"]:
                f(e)


def constants():
    import numpy as np
    cols, n = const_layout()
    c = np.zeros((P, n), np.float32)

    def put(name, value):
        c[:, cols[name][0]:cols[name][1]] = value

    r = np.arange(P)
    put("ident", np.eye(P))
    put("before", r[:, None] < r[None, :])
    put("tile_before", (r[:, None] % E == r[None, :] % E) & (r[:, None] // E < r[None, :] // E))
    put("same_expert", r[:, None] % E == np.arange(E)[None, :])
    put("first", E - np.arange(E)[None, :])
    put("steps", P * np.arange(NT)[None, :])
    put("tiles", np.arange(T0)[None, :])
    token = (np.arange(K0 * NT)[None, :] * P + r[:, None]).astype(np.uint32)
    put("token", token.view(np.float32))
    put("dump", (DUMP + np.arange(T0)[None, :] * P + r[:, None]).astype(np.uint32).view(np.float32))
    put("mask", np.where(r[None, :] > r[:, None], NEG, 0.0))
    pos = np.arange(S, dtype=np.float32)
    inv = np.exp(-np.log(10000.0) * np.arange(0, P, 2, dtype=np.float32) / P).astype(np.float32)
    ang = inv[:, None] * pos[None, :]
    pe = np.zeros((P, S), np.float32)
    pe[0::2], pe[1::2] = np.sin(ang), np.cos(ang)
    put("pe", pe)
    return c


def kernel(**inputs):
    import numpy as np
    import concourse.bacc as bacc
    from concourse.bass_utils import run_bass_kernel_spmd

    i = {k: np.asarray(v) for k, v in inputs.items()}

    def flat(x):
        return np.ascontiguousarray(x)

    def by_place(w):
        return w.reshape(-1, H0, D0).swapaxes(-1, -2).reshape(w.shape)

    arrays = {
        "x": flat(i["L0_attn_x"].reshape(NTOK, P)),
        "const": constants(),
        "Wq0": flat(by_place(i["L0_attn_Wq"])), "Wk0": flat(by_place(i["L0_attn_Wk"])),
        "Wv0": i["L0_attn_Wv"], "Wo0": i["L0_attn_Wo"],

        "bq0": flat(by_place(i["L0_attn_bq"])), "bk0": flat(by_place(i["L0_attn_bk"])),
        "bv0": i["L0_attn_bv"], "bo0": i["L0_attn_bo"],
        "gate0": flat(np.concatenate([i["L0_ffn_gate_w"], i["L0_ffn_shared_expert_gate_w"]]).T),
        "sgate": flat(i["L0_ffn_shared_gate_w"].T), "sup": flat(i["L0_ffn_shared_up_w"].T),
        "sdown": flat(i["L0_ffn_shared_down_w"].T),
        "gu0": flat(i["L0_ffn_experts_gate_up"].transpose(2, 0, 1)),
        "down0": flat(i["L0_ffn_experts_down"].transpose(0, 2, 1)),
        "Wq1": i["L1_attn_Wq"], "bq1": i["L1_attn_bq"], "Wkv1": i["L1_attn_Wkv"], "bkv1": i["L1_attn_bkv"],
        "Wo1": i["L1_attn_Wo"], "red1": flat(i["L1_ffn_wg_red"].T), "wg1": i["L1_ffn_wg"],
        "w1": i["L1_ffn_w1"], "w2": i["L1_ffn_w2"], "b1": i["L1_ffn_b1"],
        "b2": i["L1_ffn_b2"],
    }
    nc = bacc.Bacc("TRN2", target_bir_lowering=False, num_devices=1)
    aps = {k: nc.dram_tensor(k, v.shape, mybir.dt.from_np(v.dtype), kind="ExternalInput").ap() for k, v in arrays.items()}
    out = nc.dram_tensor("out", (NTOK, P), F32, kind="ExternalOutput").ap()
    build(nc, aps, out)
    r = run_bass_kernel_spmd(nc, [arrays], core_ids=[0])
    return r.results[0]["out"].reshape(B, S, P)
```
